# Optimizing a Trainium2 kernel written in Bass

```python
import numpy as np
import jax
import jax.numpy as jnp

def _softmax(x, axis=-1):
    return jax.nn.softmax(x, axis=axis)

def _gelu(x):
    return jax.nn.gelu(x, approximate=True)

def _silu(x):
    return jax.nn.silu(x)

def _sigmoid(x):
    return jax.nn.sigmoid(x)

def _layernorm(x, axis=-1, eps=1e-05):
    m = jnp.mean(x, axis=axis, keepdims=True)
    v = jnp.var(x, axis=axis, keepdims=True)
    return (x - m) / jnp.sqrt(v + eps)

def _scatter_add(tgt, idx, src, axis=0):
    return tgt.at[idx].add(src)

def _segment_sum(src, seg, n):
    return jax.ops.segment_sum(src, seg, n)
kernel_name = 'mk_flamingo_gated_d4_seqx_r8_75e971'

def setup_inputs(seed: int=0):
    np.random.seed(seed)
    _w = jnp.asarray

    def _rec_inputs():
        import jax
        import jax.numpy as jnp
        _rk = jax.random.key(seed)
        x = 0.0002417 + 0.9998 * jax.random.normal(jax.random.fold_in(_rk, 1), (16, 128, 128), jnp.float32)
        _lenS = 128 - jax.random.randint(jax.random.fold_in(_rk, 7), (16,), 0, max(1, 128 // 4) + 1, jnp.int32)
        _lenS2 = 128 - jax.random.randint(jax.random.fold_in(_rk, 8), (16,), 0, max(1, 128 // 4) + 1, jnp.int32)
        _ctx_1024P = jax.random.normal(jax.random.fold_in(_rk, 11), (16, 16, 128), jnp.float32)
        _ctx_1024c = jax.random.dirichlet(jax.random.fold_in(_rk, 511), 0.3 * jnp.ones((16,), jnp.float32), (16, 128))
        _ctx_1024t = jnp.einsum('bsk,bkd->bsd', _ctx_1024c, _ctx_1024P)
        _ctx_1024t = _ctx_1024t * jax.lax.rsqrt(jnp.mean(jnp.square(_ctx_1024t)) + 1e-12) * 0.953939
        ctx_1024 = 7.22013e-05 + 1.00017 * (_ctx_1024t + 0.3 * jax.random.normal(jax.random.fold_in(_rk, 611), (16, 128, 128), jnp.float32))
        _validS = jnp.arange(128)[None, :] < _lenS[:, None]
        _validS2 = jnp.arange(128)[None, :] < _lenS2[:, None]
        _causal = jnp.tril(jnp.ones((128, 128), dtype=bool))
        mask_BxS2_bk1 = jnp.broadcast_to(_validS2[:, :], (16, 128))
        _g = jax.random.normal(jax.random.fold_in(_rk, 9001), (2, 4), jnp.float32)
        _g = jnp.sign(_g) * jnp.maximum(jnp.abs(_g), 1.0) + (_g == 0) * 1.0
        g_xattn = _g[0]
        g_ffn = _g[1]
        return (x, ctx_1024, mask_BxS2_bk1, g_xattn, g_ffn)
    x, ctx_1024, mask_BxS2_bk1, g_xattn, g_ffn = _rec_inputs()

    def _L0_xattn_setup():
        import jax, jax.numpy as jnp
        import numpy as np
        EMBED = 128
        HEADS = 16
        HEAD_DIM = EMBED // HEADS
        key = jax.random.key(seed)
        ks = jax.random.split(key, 8)
        N, L = (2, 512)
        return {'value': jax.random.normal(ks[0], (N, L, EMBED), dtype=jnp.float32), 'key': jax.random.normal(ks[1], (N, L, EMBED), dtype=jnp.float32), 'query': jax.random.normal(ks[2], (N, L, EMBED), dtype=jnp.float32), 'Wv': jax.random.normal(ks[3], (HEAD_DIM, HEAD_DIM), dtype=jnp.float32) * HEAD_DIM ** (-0.5), 'Wk': jax.random.normal(ks[4], (HEAD_DIM, HEAD_DIM), dtype=jnp.float32) * HEAD_DIM ** (-0.5), 'Wq': jax.random.normal(ks[5], (HEAD_DIM, HEAD_DIM), dtype=jnp.float32) * HEAD_DIM ** (-0.5), 'Wo': jax.random.normal(ks[6], (EMBED, EMBED), dtype=jnp.float32) * EMBED ** (-0.5), 'bo': jnp.zeros((EMBED,), dtype=jnp.float32)}
    _L0_xattn_all = _L0_xattn_setup()
    _L0_xattn_in = {k: v for k, v in _L0_xattn_all.items() if k in ('Wv', 'Wk', 'Wq', 'Wo', 'bo')}
    del _L0_xattn_all

    def _L0_ffn_setup():
        import jax, jax.numpy as jnp
        import numpy as np
        H = 128
        I = 256
        E = 8
        B, S = (2, 128)

        def _swiglu(x, wg, wu, wd):
            return jax.nn.silu(x @ wg) * (x @ wu) @ wd
        key = jax.random.key(seed)
        ks = jax.random.split(key, 8)
        sc_h = 1.0 / np.sqrt(H)
        sc_i = 1.0 / np.sqrt(I)
        return {'hidden_states': jax.random.normal(ks[0], (B, S, H), jnp.float32), 'gate_w': jax.random.normal(ks[1], (H, E), jnp.float32) * sc_h, 'sh_gate': jax.random.normal(ks[2], (H, I), jnp.float32) * sc_h, 'sh_up': jax.random.normal(ks[3], (H, I), jnp.float32) * sc_h, 'sh_down': jax.random.normal(ks[4], (I, H), jnp.float32) * sc_i, 'rt_gate': jax.random.normal(ks[5], (E, H, I), jnp.float32) * sc_h, 'rt_up': jax.random.normal(ks[6], (E, H, I), jnp.float32) * sc_h, 'rt_down': jax.random.normal(ks[7], (E, I, H), jnp.float32) * sc_i}
    _L0_ffn_all = _L0_ffn_setup()
    _L0_ffn_in = {k: v for k, v in _L0_ffn_all.items() if k in ('gate_w', 'sh_gate', 'sh_up', 'sh_down', 'rt_gate', 'rt_up', 'rt_down')}
    del _L0_ffn_all

    def _L1_xattn_setup():
        import jax, jax.numpy as jnp
        import numpy as np
        DIM = 128
        DIM_HEAD = 64
        HEADS = 8
        INNER = DIM_HEAD * HEADS
        EPS = 1e-05

        def layernorm(x, g, b):
            mu = jnp.mean(x, axis=-1, keepdims=True)
            var = jnp.var(x, axis=-1, keepdims=True)
            return (x - mu) * jax.lax.rsqrt(var + EPS) * g + b
        key = jax.random.key(seed)
        ks = jax.random.split(key, 8)
        b, n, m = (8, 512, 64)
        x = jax.random.normal(ks[0], (b, n, DIM), dtype=jnp.float32)
        latents = jax.random.normal(ks[1], (b, m, DIM), dtype=jnp.float32)
        mask = jax.random.bernoulli(ks[2], 0.9, (b, n))
        s = DIM ** (-0.5)
        Wq = jax.random.normal(ks[3], (DIM, INNER), dtype=jnp.float32) * s
        Wkv = jax.random.normal(ks[4], (DIM, 2 * INNER), dtype=jnp.float32) * s
        Wo = jax.random.normal(ks[5], (INNER, DIM), dtype=jnp.float32) * INNER ** (-0.5)
        ln_x_g = jnp.ones((DIM,), jnp.float32)
        ln_x_b = jnp.zeros((DIM,), jnp.float32)
        ln_l_g = jnp.ones((DIM,), jnp.float32)
        ln_l_b = jnp.zeros((DIM,), jnp.float32)
        ln_o_g = jnp.ones((DIM,), jnp.float32)
        ln_o_b = jnp.zeros((DIM,), jnp.float32)
        return {'x': x, 'latents': latents, 'mask': mask, 'Wq': Wq, 'Wkv': Wkv, 'Wo': Wo, 'ln_x_g': ln_x_g, 'ln_x_b': ln_x_b, 'ln_l_g': ln_l_g, 'ln_l_b': ln_l_b, 'ln_o_g': ln_o_g, 'ln_o_b': ln_o_b}
    _L1_xattn_all = _L1_xattn_setup()
    _L1_xattn_in = {k: v for k, v in _L1_xattn_all.items() if k in ('Wq', 'Wkv', 'Wo', 'ln_x_g', 'ln_x_b', 'ln_l_g', 'ln_l_b', 'ln_o_g', 'ln_o_b')}
    del _L1_xattn_all

    def _L1_ffn_setup():
        import jax, jax.numpy as jnp
        import numpy as np

        def _ste(w, w_q):
            return w + jax.lax.stop_gradient(w_q - w)

        def quantize_w8_per(w, axis):
            amax = jnp.clip(jnp.max(jnp.abs(w), axis=axis, keepdims=True), 1e-08, None)
            scale = 127.0 / amax
            w_q = jnp.clip(jnp.round(w * scale), -128.0, 127.0) / scale
            return _ste(w, w_q)

        def quantize_a16(x):
            amax = jnp.clip(jnp.max(jnp.abs(x)), 1e-08, None)
            scale = 32767.0 / amax
            x_q = jnp.clip(jnp.round(x * scale), -32768.0, 32767.0) / scale
            return _ste(x, x_q)
        key = jax.random.key(seed)
        k1, k2, k3 = jax.random.split(key, 3)
        d_model, d_ff = (128, 512)
        x = jax.random.normal(k1, (4, 256, d_model), dtype=jnp.float32)
        W_in = jax.random.normal(k2, (d_model, d_ff), dtype=jnp.float32) / np.sqrt(d_model)
        b_in = jnp.zeros((d_ff,), dtype=jnp.float32)
        W_out = jax.random.normal(k3, (d_ff, d_model), dtype=jnp.float32) / np.sqrt(d_ff)
        b_out = jnp.zeros((d_model,), dtype=jnp.float32)
        return {'x': x, 'W_in': W_in, 'b_in': b_in, 'W_out': W_out, 'b_out': b_out}
    _L1_ffn_all = _L1_ffn_setup()
    _L1_ffn_in = {k: v for k, v in _L1_ffn_all.items() if k in ('W_in', 'b_in', 'W_out', 'b_out')}
    del _L1_ffn_all

    def _L2_xattn_setup():
        import jax, jax.numpy as jnp
        import numpy as np
        DIM = 128
        H = 16
        D = DIM // H
        SCALE = D ** (-0.5)
        LN_EPS = 1e-05

        def _layernorm(t, gamma, beta):
            mu = jnp.mean(t, axis=-1, keepdims=True)
            var = jnp.var(t, axis=-1, keepdims=True)
            return (t - mu) * jax.lax.rsqrt(var + LN_EPS) * gamma + beta
        key = jax.random.key(seed)
        ks = jax.random.split(key, 8)
        s = DIM ** (-0.5)
        return {'x': jax.random.normal(ks[0], (2, 256, DIM), dtype=jnp.float32), 'y': jax.random.normal(ks[1], (2, 256, DIM), dtype=jnp.float32), 'Wq': jax.random.normal(ks[2], (DIM, DIM), dtype=jnp.float32) * s, 'bq': jnp.zeros((DIM,), dtype=jnp.float32), 'Wkv': jax.random.normal(ks[3], (2 * DIM, DIM), dtype=jnp.float32) * s, 'bkv': jnp.zeros((2 * DIM,), dtype=jnp.float32), 'q_gamma': jnp.ones((D,), dtype=jnp.float32), 'q_beta': jnp.zeros((D,), dtype=jnp.float32), 'k_gamma': jnp.ones((D,), dtype=jnp.float32), 'k_beta': jnp.zeros((D,), dtype=jnp.float32), 'Wproj': jax.random.normal(ks[4], (DIM, DIM), dtype=jnp.float32) * s, 'bproj': jnp.zeros((DIM,), dtype=jnp.float32)}
    _L2_xattn_all = _L2_xattn_setup()
    _L2_xattn_in = {k: v for k, v in _L2_xattn_all.items() if k in ('Wq', 'bq', 'Wkv', 'bkv', 'q_gamma', 'q_beta', 'k_gamma', 'k_beta', 'Wproj', 'bproj')}
    del _L2_xattn_all

    def _L2_ffn_setup():
        import jax, jax.numpy as jnp
        import numpy as np
        DIM = 128
        HID = 256
        E = 8
        K = 2
        R = 16
        B_, S_ = (2, 128)

        def _lora_in(xf, W, b, A, B):
            base = jnp.einsum('td,ehd->teh', xf, W)
            low = jnp.einsum('ter,ehr->teh', jnp.einsum('td,erd->ter', xf, A), B)
            return base + low + b

        def _lora_out(g, W, b, A, B):
            base = jnp.einsum('teh,edh->ted', g, W)
            low = jnp.einsum('ter,edr->ted', jnp.einsum('teh,erh->ter', g, A), B)
            return base + low + b
        key = jax.random.key(seed)
        ks = jax.random.split(key, 14)
        n = lambda k, shape, scale: jax.random.normal(k, shape, jnp.float32) * scale
        inp = {'x': jax.random.normal(ks[0], (B_, S_, DIM), jnp.float32), 'Wg': n(ks[1], (E, DIM), DIM ** (-0.5)), 'W1': n(ks[2], (E, HID, DIM), DIM ** (-0.5)), 'b1': jnp.zeros((E, HID), jnp.float32), 'A1': n(ks[3], (E, R, DIM), DIM ** (-0.5)), 'B1': n(ks[4], (E, HID, R), 0.01), 'W2': n(ks[5], (E, DIM, HID), HID ** (-0.5)), 'b2': jnp.zeros((E, DIM), jnp.float32), 'A2': n(ks[6], (E, R, HID), HID ** (-0.5)), 'B2': n(ks[7], (E, DIM, R), 0.01), 'W3': n(ks[8], (E, HID, DIM), DIM ** (-0.5)), 'b3': jnp.zeros((E, HID), jnp.float32), 'A3': n(ks[9], (E, R, DIM), DIM ** (-0.5)), 'B3': n(ks[10], (E, HID, R), 0.01)}
        return inp
    _L2_ffn_all = _L2_ffn_setup()
    _L2_ffn_in = {k: v for k, v in _L2_ffn_all.items() if k in ('Wg', 'W1', 'b1', 'A1', 'B1', 'W2', 'b2', 'A2', 'B2', 'W3', 'b3', 'A3', 'B3')}
    del _L2_ffn_all

    def _L3_xattn_setup():
        import jax, jax.numpy as jnp
        import numpy as np
        NUM_HEADS = 16
        key = jax.random.key(seed)
        kq, kk, kv = jax.random.split(key, 3)
        b, s, h = (1, 512, 128)
        q = jax.random.normal(kq, (b, s, h), dtype=jnp.float32)
        k = jax.random.normal(kk, (b, s, h), dtype=jnp.float32)
        v = jax.random.normal(kv, (b, s, h), dtype=jnp.float32)
        return {'q': q, 'k': k, 'v': v}
    _L3_xattn_all = _L3_xattn_setup()
    _L3_xattn_in = {k: v for k, v in _L3_xattn_all.items() if k in ()}
    del _L3_xattn_all

    def _L3_ffn_setup():
        import jax, jax.numpy as jnp
        import numpy as np
        D = 128
        HQ = 16
        HKV = 4
        G = HQ // HKV
        K = 64
        V = 64
        E = 8
        TOPK = 2
        HID = 256
        CAP_FRAC = 0.125
        EPS = 1e-06

        def _rmsnorm(x, g):
            return x * jax.lax.rsqrt(jnp.mean(x * x, axis=-1, keepdims=True) + EPS) * g

        def _rotary_tables(t, dim):
            thetas = 10000.0 ** (-np.arange(0, dim, 2, dtype=np.float32) / dim)
            ticks = np.outer(np.arange(t, dtype=np.float32), thetas)
            ticks = np.tile(ticks, (1, 2))[None, :, None, :]
            return (jnp.asarray(np.cos(ticks)), jnp.asarray(np.sin(ticks)))

        def _neg_half(x):
            x1, x2 = jnp.split(x, 2, axis=-1)
            return jnp.concatenate([-x2, x1], axis=-1)

        def _attention(x, wq, wk, wv, wo):
            b, t, _ = x.shape
            q = (x @ wq).reshape(b, t, HQ, K)
            k = (x @ wk).reshape(b, t, HKV, K)
            v = (x @ wv).reshape(b, t, HKV, V)
            cos, sin = _rotary_tables(t, K)
            q = q * cos + _neg_half(q) * sin
            k = k * cos + _neg_half(k) * sin
            qg = q.reshape(b, t, G, HKV, K)
            scores = jnp.einsum('btghk,bThk->bghtT', qg, k)
            mask = jnp.tril(jnp.ones((t, t), bool))
            scores = jnp.where(mask, scores, -jnp.inf) / np.float32(np.sqrt(K))
            p = jax.nn.softmax(scores, axis=-1)
            out = jnp.einsum('bghtT,bThv->btghv', p, v).reshape(b, t, HQ * V)
            return out @ wo

        def _moe(x, router_w, router_b, w1, w2, w3):
            b, t, d = x.shape
            n = b * t
            xf = x.reshape(n, d)
            logits = xf @ router_w + router_b
            vals, idx = jax.lax.top_k(logits, TOPK)
            scores = jax.nn.softmax(vals, axis=-1)
            cap = int(np.floor(n * CAP_FRAC))
            oh = jax.nn.one_hot(idx, E, dtype=jnp.float32)
            pos = jnp.cumsum(jnp.cumsum(oh, axis=0), axis=1).astype(jnp.int32)
            emask = oh * (pos < cap)
            tmask = jnp.sum(emask, axis=-1)
            assign = jnp.einsum('tke,e->tk', emask, jnp.arange(E, dtype=jnp.float32)).astype(jnp.int32)
            m = jnp.max(assign, axis=-1)

            def ff(w1e, w2e, w3e):
                h = jax.nn.gelu(xf @ w2e * (xf @ w1e), approximate=False)
                return h @ w3e
            y_all = jax.vmap(ff)(w1, w2, w3)
            y = y_all[m, jnp.arange(n)]
            slot = jnp.where(tmask[..., None] > 0, y[:, None, :], xf[:, None, :])
            out = jnp.einsum('tkD,tk->tD', slot, scores)
            return out.reshape(b, t, d)
        key = jax.random.key(seed)
        ks = jax.random.split(key, 10)
        w = lambda k, shape: jax.random.normal(k, shape, jnp.float32) * 0.02
        return {'x': jax.random.normal(ks[0], (4, 64, D), jnp.float32), 'g1': jnp.ones((D,), jnp.float32), 'g2': jnp.ones((D,), jnp.float32), 'wq': w(ks[1], (D, HQ * K)), 'wk': w(ks[2], (D, HKV * K)), 'wv': w(ks[3], (D, HKV * V)), 'wo': w(ks[4], (HQ * V, D)), 'router_w': w(ks[5], (D, E)), 'router_b': jnp.zeros((E,), jnp.float32), 'w1': w(ks[6], (E, D, HID)), 'w2': w(ks[7], (E, D, HID)), 'w3': w(ks[8], (E, HID, D))}
    _L3_ffn_all = _L3_ffn_setup()
    _L3_ffn_in = {k: v for k, v in _L3_ffn_all.items() if k in ('g1', 'g2', 'wq', 'wk', 'wv', 'wo', 'router_w', 'router_b', 'w1', 'w2', 'w3')}
    del _L3_ffn_all
    return {'x': x, 'ctx_1024': ctx_1024, 'mask_BxS2_bk1': mask_BxS2_bk1, 'g_xattn': g_xattn, 'g_ffn': g_ffn, 'L0_xattn_Wv': _L0_xattn_in['Wv'], 'L0_xattn_Wk': _L0_xattn_in['Wk'], 'L0_xattn_Wq': _L0_xattn_in['Wq'], 'L0_xattn_Wo': _L0_xattn_in['Wo'], 'L0_xattn_bo': _L0_xattn_in['bo'], 'L0_ffn_gate_w': _L0_ffn_in['gate_w'], 'L0_ffn_sh_gate': _L0_ffn_in['sh_gate'], 'L0_ffn_sh_up': _L0_ffn_in['sh_up'], 'L0_ffn_sh_down': _L0_ffn_in['sh_down'], 'L0_ffn_rt_gate': _L0_ffn_in['rt_gate'], 'L0_ffn_rt_up': _L0_ffn_in['rt_up'], 'L0_ffn_rt_down': _L0_ffn_in['rt_down'], 'L1_xattn_Wq': _L1_xattn_in['Wq'], 'L1_xattn_Wkv': _L1_xattn_in['Wkv'], 'L1_xattn_Wo': _L1_xattn_in['Wo'], 'L1_xattn_ln_x_g': _L1_xattn_in['ln_x_g'], 'L1_xattn_ln_x_b': _L1_xattn_in['ln_x_b'], 'L1_xattn_ln_l_g': _L1_xattn_in['ln_l_g'], 'L1_xattn_ln_l_b': _L1_xattn_in['ln_l_b'], 'L1_xattn_ln_o_g': _L1_xattn_in['ln_o_g'], 'L1_xattn_ln_o_b': _L1_xattn_in['ln_o_b'], 'L1_ffn_W_in': _L1_ffn_in['W_in'], 'L1_ffn_b_in': _L1_ffn_in['b_in'], 'L1_ffn_W_out': _L1_ffn_in['W_out'], 'L1_ffn_b_out': _L1_ffn_in['b_out'], 'L2_xattn_Wq': _L2_xattn_in['Wq'], 'L2_xattn_bq': _L2_xattn_in['bq'], 'L2_xattn_Wkv': _L2_xattn_in['Wkv'], 'L2_xattn_bkv': _L2_xattn_in['bkv'], 'L2_xattn_q_gamma': _L2_xattn_in['q_gamma'], 'L2_xattn_q_beta': _L2_xattn_in['q_beta'], 'L2_xattn_k_gamma': _L2_xattn_in['k_gamma'], 'L2_xattn_k_beta': _L2_xattn_in['k_beta'], 'L2_xattn_Wproj': _L2_xattn_in['Wproj'], 'L2_xattn_bproj': _L2_xattn_in['bproj'], 'L2_ffn_Wg': _L2_ffn_in['Wg'], 'L2_ffn_W1': _L2_ffn_in['W1'], 'L2_ffn_b1': _L2_ffn_in['b1'], 'L2_ffn_A1': _L2_ffn_in['A1'], 'L2_ffn_B1': _L2_ffn_in['B1'], 'L2_ffn_W2': _L2_ffn_in['W2'], 'L2_ffn_b2': _L2_ffn_in['b2'], 'L2_ffn_A2': _L2_ffn_in['A2'], 'L2_ffn_B2': _L2_ffn_in['B2'], 'L2_ffn_W3': _L2_ffn_in['W3'], 'L2_ffn_b3': _L2_ffn_in['b3'], 'L2_ffn_A3': _L2_ffn_in['A3'], 'L2_ffn_B3': _L2_ffn_in['B3'], 'L3_ffn_g1': _L3_ffn_in['g1'], 'L3_ffn_g2': _L3_ffn_in['g2'], 'L3_ffn_wq': _L3_ffn_in['wq'], 'L3_ffn_wk': _L3_ffn_in['wk'], 'L3_ffn_wv': _L3_ffn_in['wv'], 'L3_ffn_wo': _L3_ffn_in['wo'], 'L3_ffn_router_w': _L3_ffn_in['router_w'], 'L3_ffn_router_b': _L3_ffn_in['router_b'], 'L3_ffn_w1': _L3_ffn_in['w1'], 'L3_ffn_w2': _L3_ffn_in['w2'], 'L3_ffn_w3': _L3_ffn_in['w3']}

def reference(x, ctx_1024, mask_BxS2_bk1, g_xattn, g_ffn, L0_xattn_Wv, L0_xattn_Wk, L0_xattn_Wq, L0_xattn_Wo, L0_xattn_bo, L0_ffn_gate_w, L0_ffn_sh_gate, L0_ffn_sh_up, L0_ffn_sh_down, L0_ffn_rt_gate, L0_ffn_rt_up, L0_ffn_rt_down, L1_xattn_Wq, L1_xattn_Wkv, L1_xattn_Wo, L1_xattn_ln_x_g, L1_xattn_ln_x_b, L1_xattn_ln_l_g, L1_xattn_ln_l_b, L1_xattn_ln_o_g, L1_xattn_ln_o_b, L1_ffn_W_in, L1_ffn_b_in, L1_ffn_W_out, L1_ffn_b_out, L2_xattn_Wq, L2_xattn_bq, L2_xattn_Wkv, L2_xattn_bkv, L2_xattn_q_gamma, L2_xattn_q_beta, L2_xattn_k_gamma, L2_xattn_k_beta, L2_xattn_Wproj, L2_xattn_bproj, L2_ffn_Wg, L2_ffn_W1, L2_ffn_b1, L2_ffn_A1, L2_ffn_B1, L2_ffn_W2, L2_ffn_b2, L2_ffn_A2, L2_ffn_B2, L2_ffn_W3, L2_ffn_b3, L2_ffn_A3, L2_ffn_B3, L3_ffn_g1, L3_ffn_g2, L3_ffn_wq, L3_ffn_wk, L3_ffn_wv, L3_ffn_wo, L3_ffn_router_w, L3_ffn_router_b, L3_ffn_w1, L3_ffn_w2, L3_ffn_w3):
    import jax
    import jax.numpy as jnp

    def _L0_xattn_ref(value, key, query, Wv, Wk, Wq, Wo, bo):
        import jax, jax.numpy as jnp
        import numpy as np
        EMBED = 128
        HEADS = 16
        HEAD_DIM = EMBED // HEADS
        N, Lq = (query.shape[0], query.shape[1])
        Lk, Lv = (key.shape[1], value.shape[1])
        v = value.reshape(N, Lv, HEADS, HEAD_DIM)
        k = key.reshape(N, Lk, HEADS, HEAD_DIM)
        q = query.reshape(N, Lq, HEADS, HEAD_DIM)
        v = jnp.einsum('nlhd,ed->nlhe', v, Wv)
        k = jnp.einsum('nlhd,ed->nlhe', k, Wk)
        q = jnp.einsum('nlhd,ed->nlhe', q, Wq)
        energy = jnp.einsum('nqhd,nkhd->nhqk', q, k)
        attention = jax.nn.softmax(energy * EMBED ** (-0.5), axis=3)
        out = jnp.einsum('nhqk,nkhd->nqhd', attention, v).reshape(N, Lq, EMBED)
        return out @ Wo.T + bo

    def _L0_ffn_ref(hidden_states, gate_w, sh_gate, sh_up, sh_down, rt_gate, rt_up, rt_down):
        import jax, jax.numpy as jnp
        import numpy as np
        H = 128
        I = 256
        E = 8
        B, S = (2, 128)

        def _swiglu(x, wg, wu, wd):
            return jax.nn.silu(x @ wg) * (x @ wu) @ wd
        b, s, h = hidden_states.shape
        x = hidden_states.reshape(-1, h)
        logits = x @ gate_w
        top_val = jnp.max(logits, axis=-1, keepdims=True)
        top_id = jnp.argmax(logits, axis=-1)
        score = jax.nn.sigmoid(top_val)
        xs = x * score
        g = jnp.einsum('th,ehi->eti', xs, rt_gate)
        u = jnp.einsum('th,ehi->eti', xs, rt_up)
        act = jax.nn.silu(g) * u
        y = jnp.einsum('eti,eih->eth', act, rt_down)
        onehot = jax.nn.one_hot(top_id, E, dtype=x.dtype)
        routed = jnp.einsum('eth,te->th', y, onehot)
        shared = _swiglu(x, sh_gate, sh_up, sh_down)
        return (shared + routed).reshape(b, s, h)

    def _L1_xattn_ref(x, latents, mask, Wq, Wkv, Wo, ln_x_g, ln_x_b, ln_l_g, ln_l_b, ln_o_g, ln_o_b):
        import jax, jax.numpy as jnp
        import numpy as np
        DIM = 128
        DIM_HEAD = 64
        HEADS = 8
        INNER = DIM_HEAD * HEADS
        EPS = 1e-05

        def layernorm(x, g, b):
            mu = jnp.mean(x, axis=-1, keepdims=True)
            var = jnp.var(x, axis=-1, keepdims=True)
            return (x - mu) * jax.lax.rsqrt(var + EPS) * g + b
        scale = DIM_HEAD ** (-0.5)
        b, m = (latents.shape[0], latents.shape[1])
        xn = layernorm(x, ln_x_g, ln_x_b)
        ln = layernorm(latents, ln_l_g, ln_l_b)
        q = ln @ Wq
        kv_in = jnp.concatenate([xn, ln], axis=1)
        kv = kv_in @ Wkv
        k, v = jnp.split(kv, 2, axis=-1)
        q = q.reshape(b, m, HEADS, DIM_HEAD).transpose(0, 2, 1, 3)
        k = k.reshape(b, k.shape[1], HEADS, DIM_HEAD).transpose(0, 2, 1, 3)
        v = v.reshape(b, v.shape[1], HEADS, DIM_HEAD).transpose(0, 2, 1, 3)
        sim = jnp.einsum('bhid,bhjd->bhij', q * scale, k) * scale
        full_mask = jnp.concatenate([mask, jnp.ones((b, m), dtype=bool)], axis=1)
        max_neg = -jnp.finfo(sim.dtype).max
        sim = jnp.where(full_mask[:, None, None, :], sim, max_neg)
        attn = jax.nn.softmax(sim.astype(jnp.float32), axis=-1).astype(sim.dtype)
        out = jnp.einsum('bhij,bhjd->bhid', attn, v)
        out = out.transpose(0, 2, 1, 3).reshape(b, m, INNER)
        out = out @ Wo
        return layernorm(out, ln_o_g, ln_o_b)

    def _L1_ffn_ref(x, W_in, b_in, W_out, b_out):
        import jax, jax.numpy as jnp
        import numpy as np

        def _ste(w, w_q):
            return w + jax.lax.stop_gradient(w_q - w)

        def quantize_w8_per(w, axis):
            amax = jnp.clip(jnp.max(jnp.abs(w), axis=axis, keepdims=True), 1e-08, None)
            scale = 127.0 / amax
            w_q = jnp.clip(jnp.round(w * scale), -128.0, 127.0) / scale
            return _ste(w, w_q)

        def quantize_a16(x):
            amax = jnp.clip(jnp.max(jnp.abs(x)), 1e-08, None)
            scale = 32767.0 / amax
            x_q = jnp.clip(jnp.round(x * scale), -32768.0, 32767.0) / scale
            return _ste(x, x_q)
        W_in_sim = quantize_w8_per(W_in, axis=0)
        W_out_sim = quantize_w8_per(W_out, axis=1)
        x_sim = quantize_a16(x)
        hidden = jax.nn.gelu(x_sim @ W_in_sim + b_in, approximate=False)
        hidden_sim = quantize_a16(hidden)
        out = hidden_sim @ W_out_sim + b_out
        return out

    def _L2_xattn_ref(x, y, Wq, bq, Wkv, bkv, q_gamma, q_beta, k_gamma, k_beta, Wproj, bproj):
        import jax, jax.numpy as jnp
        import numpy as np
        DIM = 128
        H = 16
        D = DIM // H
        SCALE = D ** (-0.5)
        LN_EPS = 1e-05

        def _layernorm(t, gamma, beta):
            mu = jnp.mean(t, axis=-1, keepdims=True)
            var = jnp.var(t, axis=-1, keepdims=True)
            return (t - mu) * jax.lax.rsqrt(var + LN_EPS) * gamma + beta
        B, N, C = x.shape
        M = y.shape[1]
        q = (x @ Wq.T + bq).reshape(B, N, H, D).transpose(0, 2, 1, 3)
        kv = (y @ Wkv.T + bkv).reshape(B, M, 2, H, D).transpose(2, 0, 3, 1, 4)
        k, v = (kv[0], kv[1])
        q = _layernorm(q, q_gamma, q_beta) * SCALE
        k = _layernorm(k, k_gamma, k_beta)
        attn = jax.nn.softmax(jnp.einsum('bhnd,bhmd->bhnm', q, k), axis=-1)
        out = jnp.einsum('bhnm,bhmd->bhnd', attn, v)
        out = out.transpose(0, 2, 1, 3).reshape(B, N, C)
        return out @ Wproj.T + bproj

    def _L2_ffn_ref(x, Wg, W1, b1, A1, B1, W2, b2, A2, B2, W3, b3, A3, B3):
        import jax, jax.numpy as jnp
        import numpy as np
        DIM = 128
        HID = 256
        E = 8
        K = 2
        R = 16
        B_, S_ = (2, 128)

        def _lora_in(xf, W, b, A, B):
            base = jnp.einsum('td,ehd->teh', xf, W)
            low = jnp.einsum('ter,ehr->teh', jnp.einsum('td,erd->ter', xf, A), B)
            return base + low + b

        def _lora_out(g, W, b, A, B):
            base = jnp.einsum('teh,edh->ted', g, W)
            low = jnp.einsum('ter,edr->ted', jnp.einsum('teh,erh->ter', g, A), B)
            return base + low + b
        orig_shape = x.shape
        xf = x.reshape(-1, x.shape[-1])
        scores = jax.nn.softmax(xf @ Wg.T, axis=-1)
        expert_weights, expert_indices = jax.lax.top_k(scores, K)
        expert_weights = expert_weights / expert_weights.sum(-1, keepdims=True)
        gates = (jax.nn.one_hot(expert_indices, E, dtype=xf.dtype) * expert_weights[..., None]).sum(axis=1)
        h1 = _lora_in(xf, W1, b1, A1, B1)
        h3 = _lora_in(xf, W3, b3, A3, B3)
        g = jax.nn.silu(h1) * h3
        y_e = _lora_out(g, W2, b2, A2, B2)
        y = jnp.einsum('te,ted->td', gates, y_e)
        return y.reshape(orig_shape)

    def _L3_xattn_ref(q, k, v):
        import jax, jax.numpy as jnp
        import numpy as np
        NUM_HEADS = 16
        b, s, hd = q.shape
        n = NUM_HEADS
        d = hd // n
        qh = q.reshape(b, s, n, d)
        kh = k.reshape(b, s, n, d)
        vh = v.reshape(b, s, n, d)
        scale = 1.0 / jnp.sqrt(jnp.float32(d))
        scores = jnp.einsum('bqnd,bknd->bnqk', qh, kh) * scale
        probs = jax.nn.softmax(scores, axis=-1)
        out = jnp.einsum('bnqk,bknd->bqnd', probs, vh)
        return out.reshape(b, s, hd)

    def _L3_ffn_ref(x, g1, g2, wq, wk, wv, wo, router_w, router_b, w1, w2, w3):
        import jax, jax.numpy as jnp
        import numpy as np
        D = 128
        HQ = 16
        HKV = 4
        G = HQ // HKV
        K = 64
        V = 64
        E = 8
        TOPK = 2
        HID = 256
        CAP_FRAC = 0.125
        EPS = 1e-06

        def _rmsnorm(x, g):
            return x * jax.lax.rsqrt(jnp.mean(x * x, axis=-1, keepdims=True) + EPS) * g

        def _rotary_tables(t, dim):
            thetas = 10000.0 ** (-np.arange(0, dim, 2, dtype=np.float32) / dim)
            ticks = np.outer(np.arange(t, dtype=np.float32), thetas)
            ticks = np.tile(ticks, (1, 2))[None, :, None, :]
            return (jnp.asarray(np.cos(ticks)), jnp.asarray(np.sin(ticks)))

        def _neg_half(x):
            x1, x2 = jnp.split(x, 2, axis=-1)
            return jnp.concatenate([-x2, x1], axis=-1)

        def _attention(x, wq, wk, wv, wo):
            b, t, _ = x.shape
            q = (x @ wq).reshape(b, t, HQ, K)
            k = (x @ wk).reshape(b, t, HKV, K)
            v = (x @ wv).reshape(b, t, HKV, V)
            cos, sin = _rotary_tables(t, K)
            q = q * cos + _neg_half(q) * sin
            k = k * cos + _neg_half(k) * sin
            qg = q.reshape(b, t, G, HKV, K)
            scores = jnp.einsum('btghk,bThk->bghtT', qg, k)
            mask = jnp.tril(jnp.ones((t, t), bool))
            scores = jnp.where(mask, scores, -jnp.inf) / np.float32(np.sqrt(K))
            p = jax.nn.softmax(scores, axis=-1)
            out = jnp.einsum('bghtT,bThv->btghv', p, v).reshape(b, t, HQ * V)
            return out @ wo

        def _moe(x, router_w, router_b, w1, w2, w3):
            b, t, d = x.shape
            n = b * t
            xf = x.reshape(n, d)
            logits = xf @ router_w + router_b
            vals, idx = jax.lax.top_k(logits, TOPK)
            scores = jax.nn.softmax(vals, axis=-1)
            cap = int(np.floor(n * CAP_FRAC))
            oh = jax.nn.one_hot(idx, E, dtype=jnp.float32)
            pos = jnp.cumsum(jnp.cumsum(oh, axis=0), axis=1).astype(jnp.int32)
            emask = oh * (pos < cap)
            tmask = jnp.sum(emask, axis=-1)
            assign = jnp.einsum('tke,e->tk', emask, jnp.arange(E, dtype=jnp.float32)).astype(jnp.int32)
            m = jnp.max(assign, axis=-1)

            def ff(w1e, w2e, w3e):
                h = jax.nn.gelu(xf @ w2e * (xf @ w1e), approximate=False)
                return h @ w3e
            y_all = jax.vmap(ff)(w1, w2, w3)
            y = y_all[m, jnp.arange(n)]
            slot = jnp.where(tmask[..., None] > 0, y[:, None, :], xf[:, None, :])
            out = jnp.einsum('tkD,tk->tD', slot, scores)
            return out.reshape(b, t, d)
        h = x + _attention(_rmsnorm(x, g1), wq, wk, wv, wo)
        return h + _moe(_rmsnorm(h, g2), router_w, router_b, w1, w2, w3)
    x = x + jnp.tanh(g_xattn[0]) * _L0_xattn_ref(ctx_1024, ctx_1024, _layernorm(x, axis=-1), L0_xattn_Wv, L0_xattn_Wk, L0_xattn_Wq, L0_xattn_Wo, L0_xattn_bo)
    x = x + jnp.tanh(g_ffn[0]) * _L0_ffn_ref(_layernorm(x, axis=-1), L0_ffn_gate_w, L0_ffn_sh_gate, L0_ffn_sh_up, L0_ffn_sh_down, L0_ffn_rt_gate, L0_ffn_rt_up, L0_ffn_rt_down)
    x = x + jnp.tanh(g_xattn[1]) * _L1_xattn_ref(ctx_1024, _layernorm(x, axis=-1), mask_BxS2_bk1, L1_xattn_Wq, L1_xattn_Wkv, L1_xattn_Wo, L1_xattn_ln_x_g, L1_xattn_ln_x_b, L1_xattn_ln_l_g, L1_xattn_ln_l_b, L1_xattn_ln_o_g, L1_xattn_ln_o_b)
    x = x + jnp.tanh(g_ffn[1]) * _L1_ffn_ref(_layernorm(x, axis=-1), L1_ffn_W_in, L1_ffn_b_in, L1_ffn_W_out, L1_ffn_b_out)
    x = x + jnp.tanh(g_xattn[2]) * _L2_xattn_ref(_layernorm(x, axis=-1), ctx_1024, L2_xattn_Wq, L2_xattn_bq, L2_xattn_Wkv, L2_xattn_bkv, L2_xattn_q_gamma, L2_xattn_q_beta, L2_xattn_k_gamma, L2_xattn_k_beta, L2_xattn_Wproj, L2_xattn_bproj)
    x = x + jnp.tanh(g_ffn[2]) * _L2_ffn_ref(_layernorm(x, axis=-1), L2_ffn_Wg, L2_ffn_W1, L2_ffn_b1, L2_ffn_A1, L2_ffn_B1, L2_ffn_W2, L2_ffn_b2, L2_ffn_A2, L2_ffn_B2, L2_ffn_W3, L2_ffn_b3, L2_ffn_A3, L2_ffn_B3)
    x = x + jnp.tanh(g_xattn[3]) * _L3_xattn_ref(_layernorm(x, axis=-1), ctx_1024, ctx_1024)
    x = x + jnp.tanh(g_ffn[3]) * _L3_ffn_ref(_layernorm(x, axis=-1), L3_ffn_g1, L3_ffn_g2, L3_ffn_wq, L3_ffn_wk, L3_ffn_wv, L3_ffn_wo, L3_ffn_router_w, L3_ffn_router_b, L3_ffn_w1, L3_ffn_w2, L3_ffn_w3)
    return x

_drawn_inputs = setup_inputs


def setup_inputs(seed=0):
    import zlib

    import numpy as np

    out = dict(_drawn_inputs(seed))
    spreads = {'L0_xattn_bo': (0.0, 0.1),
     'L1_xattn_ln_x_g': (1.0, 0.2),
     'L1_xattn_ln_x_b': (0.0, 0.1),
     'L1_xattn_ln_l_g': (1.0, 0.2),
     'L1_xattn_ln_l_b': (0.0, 0.1),
     'L1_xattn_ln_o_g': (1.0, 0.2),
     'L1_xattn_ln_o_b': (0.0, 0.1),
     'L1_ffn_b_in': (0.0, 0.1),
     'L1_ffn_b_out': (0.0, 0.1),
     'L2_xattn_bq': (0.0, 0.292),
     'L2_xattn_bkv': (0.0, 0.1),
     'L2_xattn_q_gamma': (1.0, 0.2),
     'L2_xattn_q_beta': (0.0, 0.475),
     'L2_xattn_k_gamma': (1.0, 0.2),
     'L2_xattn_k_beta': (0.0, 0.8),
     'L2_xattn_bproj': (0.0, 0.1),
     'L2_ffn_b1': (0.0, 0.277),
     'L2_ffn_b2': (0.0, 0.1),
     'L2_ffn_b3': (0.0, 0.274),
     'L3_ffn_g1': (1.0, 0.583),
     'L3_ffn_g2': (1.0, 0.2),
     'L3_ffn_router_b': (0.0, 0.1)}
    factors = {'L2_ffn_A1': 4.057,
     'L2_ffn_B1': 3.658,
     'L2_ffn_A2': 3.938,
     'L2_ffn_B2': 4.483,
     'L2_ffn_A3': 4.25,
     'L2_ffn_B3': 4.175,
     'L3_ffn_wq': 8.0,
     'L3_ffn_wk': 8.0,
     'L3_ffn_w1': 8.0,
     'L3_ffn_w2': 8.0,
     'L3_ffn_w3': 8.0}
    for name, (base, spread) in spreads.items():
        noise = np.random.default_rng([zlib.crc32(name.encode()), seed]).standard_normal(out[name].shape)
        drawn = base * np.exp(spread * noise) if base else spread * noise
        out[name] = jnp.asarray(drawn.astype(out[name].dtype))
    for name, factor in factors.items():
        out[name] = (out[name] * factor).astype(out[name].dtype)
    return out
```

```python
from contextlib import ExitStack

import concourse.bass as bass
from concourse import mybir
from concourse.alu_op_type import AluOpType as ALU
import numpy as np

F32 = mybir.dt.float32
U8 = mybir.dt.uint8
I32 = mybir.dt.int32
ACT = mybir.ActivationFunctionType
AX_X = mybir.AxisListType.X
RMAX = bass.bass_isa.ReduceOp.max

P = 128
NB = 16
T = NB * P
CH = 512
NC = T // CH
TPC = CH // P
E = 8
HALVES = 2
CAP = T // 8
ROUND = 12582912.0
BIG = 3.0e38


def constants():
    half = 32
    dim = 64
    thetas = 10000.0 ** (-np.arange(0, dim, 2, dtype=np.float32) / dim)
    ticks = np.tile(np.outer(np.arange(P, dtype=np.float32), thetas), (1, 2))
    cos, sin = np.cos(ticks).astype(np.float32), np.sin(ticks).astype(np.float32)
    rows = np.arange(P)
    c = {}
    c["ident"] = np.eye(P, dtype=np.float32)
    c["mask16"] = (rows[:, None] // 8 == np.arange(16)[None, :]).astype(np.float32)
    c["mask2"] = (rows[:, None] // 64 == np.arange(2)[None, :]).astype(np.float32)
    c["causal"] = np.where(rows[:, None] >= rows[None, :], 0.0, -BIG).astype(np.float32)
    c["upto"] = (rows[:, None] <= rows[None, :]).astype(np.float32)
    c["idx"] = np.broadcast_to(np.arange(E, dtype=np.float32) - E, (P, E)).copy()
    c["cosT"] = np.tile(cos.T, (2, 1)).copy()
    c["sinT"] = np.tile(sin.T, (2, 1)).copy()
    return c


class Chain:

    def __init__(self, engine, sem):
        self.engine, self.sem, self.n = engine, sem, 0

    def link(self, ins):
        self.n += 1
        ins.then_inc(self.sem, 1)
        self.engine.wait_ge(self.sem, self.n)


def build(nc, a, out):
    ctx = ExitStack()
    counter = [0]
    stage_sems = []

    def sb(name, shape, dt=F32):
        return ctx.enter_context(nc.sbuf_tensor(name, shape, dt))

    def sem(name):
        counter[0] += 1
        stage_sems.append(nc.alloc_semaphore(name=f"{name}_{counter[0]}"))
        return stage_sems[-1]

    def load_sem(name):
        return ctx.enter_context(nc.semaphore(name))

    def recycle():
        nc.clear_and_free_semaphores(stage_sems)
        stage_sems.clear()
        nc.all_engine_barrier()

    def rows(n):
        return [P, n]

    with ctx:
        ps = [ctx.enter_context(nc.psum_tensor(f"bank{i}", [P, CH], F32)) for i in range(8)]

        x = sb("x", [P, NB, P])
        ctx_tok = sb("ctx_tok", [P, NB, P])
        ctxT = sb("ctxT", [P, T])
        xn = sb("xn", [P, NB, P])
        xT = sb("xT", [P, T])
        qT = sb("qT", [P, T])
        kT = sb("kT", [P, T])
        v_tok = sb("v_tok", [P, NB, P])
        work = sb("work", [P, 16384 // 4 * 1])
        kv = sb("kv", [P, 8192])
        arena_a = sb("arena_a", [P, 3, E, 256])
        arena_b = sb("arena_b", [P, 3, E, 256])
        shw = v_tok[:, 0:6, :].rearrange("p (w a) d -> p w (a d)", w=3)
        att = sb("att", [P, 4096])
        wsq = sb("wsq", [P, 8, P])
        bias = sb("bias", [P, 7, P])
        cols = sb("cols", [P, 48])
        ident = sb("ident", [P, P])
        mask16 = sb("mask16", [P, 16])
        mask2 = sb("mask2", [P, 2])
        causal = sb("causal", [P, P])
        upto = sb("upto", [P, P])
        ones = sb("ones", [P, P])
        cosT = sb("cosT", [P, P])
        sinT = sb("sinT", [P, P])
        idx = sb("idx", [P, E])
        router = sb("router", [P, 3, E])
        rbias = sb("rbias", [P, E])
        b2 = sb("b2", [E, P])
        m8 = sb("m8", [P, NB, P // 4], I32)
        stat = sb("stat", [P, 12, 16])
        gates = sb("gates", [P, NB, E + 1])
        pt = sb("pt", [P, 2, CH])
        q_s = sb("q_s", [P, 2, CH])
        oT_s = sb("oT_s", [P, 1024])
        stage = sb("stage", [P, 2, 256])
        tiny = sb("tiny", [P, 64])

        SQ = {n: i for i, n in enumerate(["l0q", "l0k", "l0v", "l0o", "l2q", "l2k", "l2v", "l2o"])}
        BIAS = {n: i for i, n in enumerate(["l0o", "l2q", "l2k", "l2o", "lno_g", "lno_b", "g2"])}
        w_sq = {n: wsq[:, i, :] for n, i in SQ.items()}
        b_row = {n: bias[:, i, :] for n, i in BIAS.items()}

        tg = {("x", l): cols[:, l:l + 1] for l in range(4)} | {("f", l): cols[:, 4 + l:5 + l] for l in range(4)}
        col = {n: cols[:, 8 + i:9 + i] for i, n in enumerate(
            ["lnx_g", "lnx_b", "lnl_g", "lnl_b", "l2q_g", "l2q_b", "l2k_g", "l2k_b", "g1", "g2",
             "b_in0", "b_in1", "b_in2", "b_in3"])}
        b1_cols = sb("b1_cols", [P, E, 2])
        b1_half = sb("b1_half", [P, E, 2])
        b3_cols = sb("b3_cols", [P, E, 2])
        bo1_row = sb("bo1_row", [P, P])

        l1q = att[:, 0:512]
        l1kv = att[:, 512:1536]
        l1o = att[:, 1536:2048].rearrange("p (g d) -> p g d", g=4)
        winT = att[:, 2048:2560].rearrange("p (g d) -> p g d", g=4)
        wout = att[:, 2560:3072].rearrange("p (g d) -> p g d", g=4)
        win_q = att[:, 3072:3584]
        wout_q = att[:, 3584:4096].rearrange("p (g d) -> p g d", g=4)
        l3q = att[:, 0:1024]
        l3q_rot = att[:, 1024:2048]
        l3k = att[:, 2048:2304]
        l3k_rot = att[:, 2304:2560]
        l3v = att[:, 2560:2816]
        l3o = att[:, 2816:3840].rearrange("p (t d) -> p t d", t=8)

        def bc(ap, n):
            return ap.unsqueeze(2).broadcast_to([ap.shape[0], ap.shape[1], n])

        def flat(t):
            return t[:].rearrange("p b d -> p (b d)")

        def over(ap, n):
            return ap.unsqueeze(1).broadcast_to([ap.shape[0], n, ap.shape[1]])

        class Norm:

            def __init__(self, name):
                self.cent, self.sq, self.var, self.rstd = (
                    sem(f"{name}_centred"), sem(f"{name}_squared"), sem(f"{name}_variance"), sem(f"{name}_rstd"))
                self.n = {"v": 0, "s": 0, "g": 0}

            def vector(self, v, chain, src, dst, eps, centre=True, sq=None):
                self.n["v"] += 1
                k = self.n["v"]
                sq = v_sq if sq is None else sq
                if centre:
                    chain.link(v.tensor_reduce(stat[:, 0, :], src, AX_X, ALU.add))
                    chain.link(v.tensor_scalar(stat[:, 1, :], stat[:, 0, :], 1.0 / P, None, ALU.mult))
                    chain.link(v.tensor_tensor(dst, src, bc(stat[:, 1, :], P), ALU.subtract))
                    src = dst
                v.drain().then_inc(self.cent, 1)
                v.wait_ge(self.sq, k)
                chain.link(v.tensor_reduce(stat[:, 2, :], sq, AX_X, ALU.add))
                v.tensor_scalar(stat[:, 3, :], stat[:, 2, :], 1.0 / P, eps, ALU.mult, ALU.add)\
                    .then_inc(self.var, 1)
                v.wait_ge(self.rstd, k)
                chain.link(v.tensor_tensor(dst, src, bc(stat[:, 4, :], P), ALU.mult))

            def scalar(self, s, src, sq=None):
                self.n["s"] += 1
                s.wait_ge(self.cent, self.n["s"])
                s.activation(v_sq if sq is None else sq, src, ACT.Square).then_inc(self.sq, 1)

            def gpsimd(self, g):
                self.n["g"] += 1
                g.wait_ge(self.var, self.n["g"])
                g.tensor_tensor(stat[:, 4, :], stat[:, 3, :], stat[:, 5, :], ALU.pow).then_inc(self.rstd, 1)

        v_sq = work[:, 0:2048].rearrange("p (b d) -> p b d", b=NB)
        work2 = work[:, 2048:4096].rearrange("p (b d) -> p b d", b=NB)

        def transposes(pe, src, bank, c):
            for t in range(TPC):
                ins = pe.transpose(ps[bank][:, t * P:(t + 1) * P], src[:, c * TPC + t, :], ident[:])
            return ins

        s_load = load_sem("first_loads")
        s_w = {n: load_sem(f"{n}_loaded") for n in ("a", "b", "att", "misc", "lora", "att3", "a3")}
        n_load = 0
        loads = []

        def bcast(name, width):
            return a[name].broadcast_to([P, width]) if a[name].shape[0] == 1 else a[name]

        with nc.Block() as block:
            @block.sync
            def _(sp):
                sp.dma_start(x[:], a["x"].rearrange("b p d -> p b d")).then_inc(s_load, 16)
                sp.dma_start(ctxT[:], a["ctxT"]).then_inc(s_load, 16)
                sp.dma_start(wsq[:], a["squares"].rearrange("n p d -> p n d")).then_inc(s_load, 16)
                sp.dma_start(bias[:], a["bias_rows"]).then_inc(s_load, 16)
                sp.dma_start(cols[:, 8:22], a["cols"]).then_inc(s_load, 16)
                sp.dma_start(cols[:, 0:8], a["gate_cols"]).then_inc(s_load, 16)
                for name, dst in (("ident", ident), ("mask16", mask16), ("mask2", mask2), ("causal", causal),
                                  ("upto", upto), ("cosT", cosT), ("sinT", sinT), ("idx", idx),
                                  ("rbias", rbias), ("l2_b2", b2), ("b1c", b1_cols), ("b3c", b3_cols),
                                  ("bo1", bo1_row), ("router", router)):
                    sp.dma_start(dst[:], a[name]).then_inc(s_load, 16)
                sp.dma_start(ctx_tok[:], a["ctx"].rearrange("b p d -> p b d")).then_inc(s_load, 16)
                sp.dma_start(m8[:], a["mask8"]).then_inc(s_load, 16)

            @block.scalar
            def _(s):
                s.dma_start(arena_b[:, 0], a["l2_w1T"]).then_inc(s_w["lora"], 16)
                s.dma_start(arena_b[:, 1], a["l2_w3T"]).then_inc(s_w["lora"], 16)
                s.dma_start(arena_b[:, 2], a["l2_w2T"]).then_inc(s_w["lora"], 16)
                for i, name in enumerate(("l2_a1", "l2_a3", "l2_b2T")):
                    s.dma_start(work[0:16, i * 1024:(i + 1) * 1024], a[name]).then_inc(s_w["lora"], 16)
                for i, name in enumerate(("l2_b1T", "l2_b3T", "l2_a2")):
                    s.dma_start(kv[0:16, i * 2048:(i + 1) * 2048], a[name]).then_inc(s_w["lora"], 16)
                s.dma_start(arena_a[:, 0], a["l0_gate"].rearrange("e h i -> h e i")).then_inc(s_w["a"], 16)
                s.dma_start(arena_a[:, 1], a["l0_up"].rearrange("e h i -> h e i")).then_inc(s_w["a"], 16)
                s.dma_start(arena_a[:, 2].rearrange("p e (a d) -> p e a d", a=2),
                            a["l0_down"].rearrange("e (a p) d -> p e a d", p=P)).then_inc(s_w["a"], 16)
                s.dma_start(l1q, a["l1_wq"]).then_inc(s_w["att"], 16)
                s.dma_start(l1kv, a["l1_wkv"]).then_inc(s_w["att"], 16)
                s.dma_start(l1o, a["l1_wo"].rearrange("(g p) d -> p g d", p=P)).then_inc(s_w["att"], 16)
                s.dma_start(winT, a["l1_winT"].rearrange("(g p) d -> p g d", p=P)).then_inc(s_w["att"], 16)
                s.dma_start(wout, a["l1_wout"].rearrange("(g p) d -> p g d", p=P)).then_inc(s_w["att"], 16)

            @block.gpsimd
            def _(g):
                g.memset(stat[:, 5, :], -0.5)
                g.memset(ones[:], 1.0)

        s_prod, s_sum = sem("lora_product"), sem("lora_added")
        with nc.Block() as block:
            n_first = 22

            @block.tensor
            def _(pe):
                pe.wait_ge(s_w["lora"], 16 * 9)
                for m in range(3):
                    for e in range(E):
                        u = m * E + e
                        if u >= 2:
                            pe.wait_ge(s_sum, u - 1)
                        o = ps[u % 2]
                        fac = kv[0:16, m * 2048 + e * 256:m * 2048 + (e + 1) * 256]
                        if m < 2:
                            ins = pe.matmul(o[:, 0:256], work[0:16, m * 1024 + e * P:m * 1024 + (e + 1) * P], fac,
                                            start=True, stop=True)
                        else:
                            for h in range(HALVES):
                                ins = pe.matmul(o[:, h * P:(h + 1) * P], fac[:, h * P:(h + 1) * P],
                                                work[0:16, 2048 + e * P:2048 + (e + 1) * P],
                                                start=True, stop=True)
                        ins.then_inc(s_prod, 1)

            @block.vector
            def _(v):
                order = [0, 1, 2]
                for m in order:
                    for e in range(E):
                        u = m * E + e
                        v.wait_ge(s_prod, u + 1)
                        v.tensor_tensor(arena_b[:, m, e, :], arena_b[:, m, e, :], ps[u % 2][:, 0:256], ALU.add)\
                            .then_inc(s_sum, 1)

            @block.scalar
            def _(s):
                s.wait_ge(s_load, 16 * n_first)
                s_tanh = sem("gates_tanh")
                s.activation(cols[:, 0:8], cols[:, 0:8], ACT.Tanh).then_inc(s_tanh, 1)
                s.activation(b1_half[:], b1_cols[:], ACT.Copy, scale=0.5).then_inc(s_tanh, 1)

        def zero_values(g):
            return g.memset(kv[:, 4096:8192], 0.0)

        def attention_inputs(layer):
            norm = Norm(f"l{layer}")
            s_xn, s_xt, s_xe, s_pr, s_ev = (sem("normed"), sem("turned"), sem("turned_copied"),
                                            sem("projected"), sem("projected_copied"))
            s_chain, s_bias, s_h = sem("vector_step"), sem("bias_row"), sem("head_norm")
            hn = Norm(f"l{layer}_heads")

            with nc.Block() as block:
                @block.vector
                def _(v):
                    ch = Chain(v, s_chain)
                    norm.vector(v, ch, x[:], xn[:], 1e-5)
                    v.drain().then_inc(s_xn, 1)
                    if layer == 0:
                        for c in range(NC):
                            v.wait_ge(s_pr, 2 * c + 1)
                            v.tensor_copy(kT[:, c * CH:(c + 1) * CH], ps[4][:]).then_inc(s_ev, 1)
                    if layer == 2:
                        v.wait_ge(s_bias, 1)
                        v.tensor_tensor(b_row["l2o"], b_row["l2o"], ps[7][:, 0:P], ALU.add).then_inc(s_bias, 1)

                @block.gpsimd
                def _(g):
                    norm.gpsimd(g)
                    zero_values(g)
                    if layer != 3:
                        g.wait_ge(s_xn, 1)
                        if layer == 2:
                            g.wait_ge(s_bias, 2)
                        name = f"l{layer}o"
                        g.tensor_scalar(b_row[name], b_row[name], tg["x", layer], None, ALU.mult).then_inc(s_h, 1)
                        g.wait_ge(s_h, 1)
                        g.tensor_tensor(x[:], x[:], over(b_row[name], NB), ALU.add).then_inc(s_h, 1)

                @block.tensor
                def _(pe):
                    if layer == 0:
                        for c in range(NC):
                            if c >= 1:
                                pe.wait_ge(s_ev, c)
                            pe.matmul(ps[4][:], w_sq["l0k"], ctxT[:, c * CH:(c + 1) * CH], start=True, stop=True)\
                                .then_inc(s_pr, 1)
                            if c >= 1:
                                pe.wait_ge(s_xe, c)
                            for t in range(TPC):
                                ins = pe.matmul(ps[5][:, t * P:(t + 1) * P],
                                                ctxT[:, c * CH + t * P:c * CH + (t + 1) * P], w_sq["l0v"],
                                                start=True, stop=True)
                            ins.then_inc(s_pr, 1)
                    if layer == 2:
                        pe.wait_ge(s_w["misc"], 16 * 4)
                        pe.matmul(ps[7][:, 0:P], xT[:, 0:P], w_sq["l2o"], start=True, stop=True).then_inc(s_bias, 1)
                    pe.wait_ge(s_xn, 1)
                    for c in range(NC):
                        transposes(pe, xn[:], c, c).then_inc(s_xt, 1)
                    if layer == 0:
                        for c in range(NC):
                            pe.wait_ge(s_xe, NC + c + 1)
                            if c >= 2:
                                pe.wait_ge(s_xe, 2 * NC + c - 1)
                            pe.matmul(ps[6 + c % 2][:], w_sq["l0q"], xT[:, c * CH:(c + 1) * CH],
                                      start=True, stop=True).then_inc(s_pr, 1)

                @block.scalar
                def _(s):
                    norm.scalar(s, xn[:])
                    if layer == 0:
                        for c in range(NC):
                            s.wait_ge(s_pr, 2 * c + 2)
                            s.activation(v_tok[:, c * TPC:(c + 1) * TPC, :],
                                         ps[5][:].rearrange("p (t d) -> p t d", t=TPC), ACT.Copy).then_inc(s_xe, 1)
                    dst = qT if layer == 3 else xT
                    for c in range(NC):
                        s.wait_ge(s_xt, c + 1)
                        s.activation(dst[:, c * CH:(c + 1) * CH], ps[c][:], ACT.Copy).then_inc(s_xe, 1)
                    if layer == 0:
                        for c in range(NC):
                            s.wait_ge(s_pr, 2 * NC + c + 1)
                            s.activation(qT[:, c * CH:(c + 1) * CH], ps[6 + c % 2][:], ACT.Copy).then_inc(s_xe, 1)

        def l2_heads():
            s_pr, s_ev, s_vev, s_t, s_te = (sem("l2_projected"), sem("l2_biased"), sem("l2_values_copied"),
                                            sem("l2_turned"), sem("l2_turned_copied"))
            s_chain, s_sq, s_cent, s_var, s_rs = (sem("vector_step"), sem("heads_squared"), sem("heads_centred"),
                                                  sem("heads_variance"), sem("heads_rstd"))
            G = NB * 16
            w2 = flat(work2)
            mean, var, root, rstd, tmp = (w2[:, 512 * i:512 * i + 2 * G] for i in (0, 1, 2, 3, 0))
            squares = [v_sq, kT[:].rearrange("p (b d) -> p b d", b=NB)]
            rows_of = {0: xn, 1: v_tok}

            def grouped(t):
                return t[:].rearrange("p b (h d) -> p (b h) d", d=8)

            with nc.Block() as block:
                @block.tensor
                def _(pe):
                    for i, (src, w) in enumerate(((xT, "l2q"), (ctxT, "l2k"))):
                        for c in range(NC):
                            u = i * NC + c
                            if u >= 2:
                                pe.wait_ge(s_ev, u - 1)
                            for t in range(TPC):
                                at = c * CH + t * P
                                ins = pe.matmul(ps[u % 2][:, t * P:(t + 1) * P], src[:, at:at + P], w_sq[w],
                                                start=True, stop=True)
                            ins.then_inc(s_pr, 1)
                    for i in range(2):
                        pe.wait_ge(s_cent, 3 + i)
                        for c in range(NC):
                            if i:
                                pe.wait_ge(s_te, c + 1)
                            transposes(pe, rows_of[i][:], 2 + c, c).then_inc(s_t, 1)
                    pe.wait_ge(s_te, 2 * NC)
                    for c in range(NC):
                        for t in range(TPC):
                            at = c * CH + t * P
                            ins = pe.matmul(ps[2 + c][:, t * P:(t + 1) * P], ctxT[:, at:at + P], w_sq["l2v"],
                                            start=True, stop=True)
                        ins.then_inc(s_t, 1)

                @block.vector
                def _(v):
                    ch = Chain(v, s_chain)
                    for i, b in ((0, "l2q"), (1, "l2k")):
                        for c in range(NC):
                            u = i * NC + c
                            v.wait_ge(s_pr, u + 1)
                            v.tensor_tensor(rows_of[i][:, c * TPC:(c + 1) * TPC, :],
                                            ps[u % 2][:].rearrange("p (t d) -> p t d", t=TPC),
                                            over(b_row[b], TPC), ALU.add).then_inc(s_ev, 1)
                    v.wait_ge(s_ev, 2 * NC)
                    for i in range(2):
                        r, m = grouped(rows_of[i]), mean[:, i * G:(i + 1) * G]
                        ch.link(v.tensor_reduce(m, r, AX_X, ALU.add))
                        ch.link(v.tensor_scalar(m, m, 1.0 / 8, None, ALU.mult))
                        v.tensor_tensor(r, r, bc(m, 8), ALU.subtract).then_inc(s_cent, 1)
                    for i in range(2):
                        v.wait_ge(s_sq, i + 1)
                        ch.link(v.tensor_reduce(var[:, i * G:(i + 1) * G],
                                                squares[i].rearrange("p b (h d) -> p (b h) d", d=8), AX_X, ALU.add))
                    v.tensor_scalar(var, var, 1.0 / 8, 1e-5, ALU.mult, ALU.add).then_inc(s_var, 1)
                    v.wait_ge(s_rs, 1)
                    ch.link(v.reciprocal(rstd, root))
                    ch.link(v.tensor_tensor(tmp, rstd, rstd, ALU.mult))
                    ch.link(v.tensor_tensor(tmp, tmp, var, ALU.mult))
                    ch.link(v.tensor_scalar(tmp, tmp, -0.5, 1.5, ALU.mult, ALU.add))
                    ch.link(v.tensor_tensor(rstd, rstd, tmp, ALU.mult))
                    for i in range(2):
                        r = grouped(rows_of[i])
                        v.tensor_tensor(r, r, bc(rstd[:, i * G:(i + 1) * G], 8), ALU.mult).then_inc(s_cent, 1)

                @block.scalar
                def _(s):
                    for i in range(2):
                        s.wait_ge(s_cent, i + 1)
                        s.activation(squares[i], rows_of[i][:], ACT.Square).then_inc(s_sq, 1)
                    s.wait_ge(s_var, 1)
                    s.activation(root, var, ACT.Sqrt).then_inc(s_rs, 1)
                    for i, (dst, g_, b_) in enumerate(((qT, "l2q_g", "l2q_b"), (kT, "l2k_g", "l2k_b"))):
                        for c in range(NC):
                            s.wait_ge(s_t, i * NC + c + 1)
                            s.activation(dst[:, c * CH:(c + 1) * CH], ps[2 + c][:], ACT.Identity,
                                         scale=col[g_], bias=col[b_]).then_inc(s_te, 1)
                    for c in range(NC):
                        s.wait_ge(s_t, 2 * NC + c + 1)
                        s.activation(v_tok[:, c * TPC:(c + 1) * TPC, :],
                                     ps[2 + c][:].rearrange("p (t d) -> p t d", t=TPC), ACT.Copy).then_inc(s_vev, 1)

        class Heads16:
            heads = 4
            tiles = 1
            mask = None

            def __init__(self, layer, scale, values, out_w):
                self.layer, self.scale, self.values, self.out_w = layer, scale, values, out_w
                self.keys_src = ctxT if layer == 3 else kT

            def km(self, par):
                return kv[:, par * 2048:(par + 1) * 2048].rearrange("p (h k) -> p h k", h=16)

            def vm(self, par):
                return kv[:, 4096 + par * 2048:4096 + (par + 1) * 2048]

            def scores(self, pe, bank, par, g):
                return pe.matmul(bank[:], q_s[:, par, 0:P],
                                 kv[:, par * 2048 + g * CH:par * 2048 + (g + 1) * CH], start=True, stop=True)

            def pv(self, pe, par, g, pt_g):
                for j in range(4):
                    h = 4 * g + j
                    ins = pe.matmul(ps[4 + par][:, 0:P], self.vm(par)[:, h * P:(h + 1) * P], pt_g[:, j * P:(j + 1) * P],
                                    start=(h == 0), stop=(h == 15))
                return ins

            def setup(self):
                self.s_km, self.s_q, self.s_vm = sem("keys_masked"), sem("queries_staged"), sem("values_placed")

            def scores_ready(self, pe, b, g):
                if g == 0:
                    pe.wait_ge(self.s_km, b + 1)
                    pe.wait_ge(self.s_q, b + 1)

            def values_ready(self, pe, b):
                pe.wait_ge(self.s_vm, b + 1)

            def mask_keys(self, gp, n, par, first, cnt):
                if not first:
                    gp.wait_ge(cnt["scores"], 4 * (n - 1))
                gp.tensor_tensor(self.km(par), over(self.keys_src[:, bass.ds(n * P, P)], 16), bc(mask16[:], P),
                                 ALU.mult).then_inc(self.s_km, 1)

            def stage_queries(self, s, n, par, first, cnt):
                if not first:
                    s.wait_ge(cnt["scores"], 4 * (n - 1))
                s.activation(q_s[:, par, 0:P], qT[:, bass.ds(n * P, P)], ACT.Copy).then_inc(self.s_q, 1)

            def place_values(self, s, n, par, first, cnt):
                if not first:
                    s.wait_ge(cnt["pv"], 4 * (n - 1))
                s.activation(self.diag(par), self.values[:, bass.ds(n, 1), :]
                             .rearrange("p o (h d) -> p (o h) d", h=16), ACT.Copy).then_inc(self.s_vm, 1)

            pe_fronts = dve_fronts = ()
            out_banks = 2
            scalar_sums = False

            @property
            def pool_fronts(self):
                return ((1, 0, self.mask_keys),)

            @property
            def act_fronts(self):
                return ((1, 1, self.stage_queries), (0, 1, self.place_values))

            def out_bank(self, par, k):
                return ps[4 + par]

            def diag(self, par):
                return strided(self.vm(par), [(P + 8, 16), (1, 8)])

        def strided(ap, dims):
            return bass.AP(tensor=ap.tensor, offset=ap.offset, ap=[ap.ap[0]] + [[step, n] for step, n in dims])

        def attention(spec):
            spec.setup()
            s_s, s_mx, s_sub, s_exp, s_sum, s_r, s_n = (
                sem("scores"), sem("maxima"), sem("shifted"), sem("exponentials"), sem("sums"),
                sem("reciprocals"), sem("probabilities"))
            s_t, s_tev, s_pv, s_oev, s_y, s_res = (sem("turned"), sem("turned_copied"), sem("products"),
                                                   sem("output_copied"), sem("projected"), sem("residual"))
            s_add = sem("masked")
            cnt = {"scores": s_s, "pv": s_pv}
            nh = spec.heads
            prob = [work[:, i * 2048:(i + 1) * 2048] for i in range(2)]
            mx, sm, rc = tiny[:, 0:16], tiny[:, 16:32], tiny[:, 32:48]
            nt = spec.tiles

            def unit(par, g):
                return prob[par][:, g * CH:(g + 1) * CH].rearrange("p (h k) -> p h k", h=nh)

            def at(buf, g):
                return buf[:, 4 * g:4 * g + nh]

            def pe_step(pe, b, par, g, do):
                u = 4 * b + g
                if "back" in do:
                    pe.wait_ge(s_n, u - 3)
                    if not ("first_back" in do and g == 0):
                        pe.wait_ge(s_tev, u - 4)
                    for j in range(4):
                        ins = pe.transpose(ps[2][:, j * P:(j + 1) * P],
                                           prob[1 - par][:, g * CH + j * P:g * CH + (j + 1) * P], ident[:])
                    ins.then_inc(s_t, 1)
                if "scores" in do:
                    spec.scores_ready(pe, b, g)
                    if not ("first" in do and g < 2):
                        pe.wait_ge(s_sub, u - 1)
                    spec.scores(pe, ps[g % 2], par, g).then_inc(s_s, 1)
                if ("back" in do and g) or ("out" in do and g == 0):
                    pb, pg = (1 - par, g - 1) if g else (par, 3)
                    pe.wait_ge(s_tev, u - 4)
                    if pg == 0:
                        spec.values_ready(pe, b - 1)
                        if spec.out_banks == 2 and not ("first_back" in do or "first_out" in do):
                            pe.wait_ge(s_oev, b - 2)
                        if spec.out_banks == 1 and not "first_back" in do:
                            pe.wait_ge(s_oev, b - 1)
                    spec.pv(pe, pb, pg, pt[:, (g + 1) % 2, :]).then_inc(s_pv, 1)
                if "out" in do and g == 3:
                    pe.wait_ge(s_oev, b - 1)
                    if not "first_out" in do:
                        pe.wait_ge(s_res, b - 2)
                    for t in range(nt):
                        ins = pe.matmul(ps[3][:, 0:P], oT_s[:, t * P:(t + 1) * P], spec.out_w(t),
                                        start=(t == 0), stop=(t == nt - 1))
                    ins.then_inc(s_y, 1)
                hooks(spec.pe_fronts, pe, b, par, g, do)

            def dve_step(v, b, par, g, do):
                u = 4 * b + g
                hooks(spec.dve_fronts, v, b, par, g, do)
                if "scores" in do:
                    bank = ps[g % 2][:].rearrange("p (h k) -> p h k", h=nh)
                    v.wait_ge(s_s, u + 1)
                    if spec.mask is not None:
                        dst, m = spec.mask(bank, b)
                        v.tensor_tensor(dst, dst, m, ALU.add).then_inc(s_add, 1)
                        v.wait_ge(s_add, u + 1)
                    v.tensor_reduce(at(mx, g), bank, AX_X, ALU.max).then_inc(s_mx, 1)
                    v.wait_ge(s_mx, u + 1)
                    v.tensor_tensor(unit(par, g), bank, bc(at(mx, g), CH // nh), ALU.subtract).then_inc(s_sub, 1)
                if ("scores" in do and not ("first" in do and g == 0)) or ("drain" in do and g == 0):
                    pg = (g - 1) % 4
                    pp = par if g else 1 - par
                    v.wait_ge(s_exp, u)
                    if not spec.scalar_sums:
                        v.tensor_reduce(at(sm, pg), unit(pp, pg), AX_X, ALU.add).then_inc(s_sum, 1)
                        v.wait_ge(s_sum, u)
                    v.reciprocal(at(rc, pg), at(sm, pg)).then_inc(s_r, 1)
                if "out" in do and g == 3:
                    v.wait_ge(s_y, b - 1)
                    xb = spec.dst[:, bass.ds(b - 2, 1), :].rearrange("p o d -> p (o d)")
                    spec.residual(v, xb, ps[3][:, 0:P]).then_inc(s_res, 1)

            def act_step(s, b, par, g, do):
                u = 4 * b + g
                if "back" in do:
                    s.wait_ge(s_t, u - 3)
                    if not ("first_back" in do and g < 2):
                        s.wait_ge(s_pv, u - 5)
                    s.activation(pt[:, g % 2, :], ps[2][:], ACT.Copy).then_inc(s_tev, 1)
                hooks(spec.act_fronts, s, b, par, g, do)
                if "scores" in do:
                    s.wait_ge(s_sub, u + 1)
                    if spec.scalar_sums:
                        for h in range(nh):
                            w = unit(par, g)[:, h, :]
                            ins = s.activation(w, w, ACT.Exp, scale=spec.scale,
                                               accum_out=sm[:, 4 * g + h:4 * g + h + 1])
                        ins.then_inc(s_exp, 1)
                    else:
                        s.activation(unit(par, g), unit(par, g), ACT.Exp, scale=spec.scale).then_inc(s_exp, 1)
                if "out" in do and g == 0:
                    s.wait_ge(s_pv, 4 * (b - 1))
                    if not "first_out" in do:
                        s.wait_ge(s_y, b - 2)
                    for k in range((nt + 3) // 4):
                        w = min(nt, 4) * P
                        ins = s.activation(oT_s[:, k * CH:k * CH + w], spec.out_bank(par, k)[:, 0:w], ACT.Copy)
                    ins.then_inc(s_oev, 1)

            def pool_step(gp, b, par, g, do):
                u = 4 * b + g
                if ("scores" in do and not ("first" in do and g == 0)) or ("drain" in do and g == 0):
                    pg = (g - 1) % 4
                    pp = par if g else 1 - par
                    gp.wait_ge(s_r, u)
                    w = unit(pp, pg)
                    gp.tensor_tensor(w, w, bc(at(rc, pg), CH // nh), ALU.mult).then_inc(s_n, 1)
                hooks(spec.pool_fronts, gp, b, par, g, do)

            def hooks(table, eng, b, par, g, do):
                for ahead, step, f in table:
                    if step != g:
                        continue
                    if isinstance(b, int):
                        if 0 <= b + ahead < NB:
                            f(eng, b + ahead, (par + ahead) % 2, b + ahead < 2, cnt)
                    else:
                        f(eng, b + ahead, (par + ahead) % 2, False, cnt)

            def phases(b):
                do = set()
                if 0 <= b < NB:
                    do |= {"scores"}
                if b == 0:
                    do |= {"first"}
                if 1 <= b <= NB:
                    do |= {"back"}
                if b == 1:
                    do |= {"first_back"}
                if b == NB:
                    do |= {"drain"}
                if b >= 2:
                    do |= {"out"}
                if b == 2:
                    do |= {"first_out"}
                return do

            def run(eng, step):
                for b in (-2, -1, 0, 1, 2):
                    for g in range(4):
                        step(eng, b, b % 2, g, phases(b))
                with eng.Fori(0, 5) as i:
                    for k in range(2):
                        for g in range(4):
                            step(eng, 2 * i + (3 + k), (3 + k) % 2, g, phases(3))
                for b in (13, 14, 15, 16, 17):
                    for g in range(4):
                        step(eng, b, b % 2, g, phases(b))

            with nc.Block() as block:
                @block.tensor
                def _(pe):
                    run(pe, pe_step)

                @block.vector
                def _(v):
                    run(v, dve_step)

                @block.scalar
                def _(s):
                    run(s, act_step)

                @block.gpsimd
                def _(gp):
                    run(gp, pool_step)

        def add_to(spec, dst, gate=None):
            spec.dst = dst
            if gate is None:
                spec.residual = lambda v, o, y: v.tensor_copy(o, y)
            elif gate == 1:
                spec.residual = lambda v, o, y: v.tensor_tensor(o, y, o, ALU.add)
            else:
                spec.residual = lambda v, o, y: v.scalar_tensor_tensor(
                    out=o, in0=y, scalar=gate, in1=o, op0=ALU.mult, op1=ALU.add)

        rt = work[:, 0:2048].rearrange("p (s n) -> p s n", s=16)

        def slot(i):
            return rt[:, i, :].rearrange("p (b e) -> p b e", e=E)

        def choose(v, ch, logits, best, onehot, tmp):
            ch.link(v.tensor_reduce(best, logits, AX_X, ALU.max))
            ch.link(v.tensor_tensor(tmp, logits, bc(best, E), ALU.is_equal))
            ch.link(v.tensor_tensor(tmp, tmp, over(idx[:], NB), ALU.mult))
            ch.link(v.tensor_reduce(stat[:, 6, :], tmp, AX_X, ALU.min))
            ch.link(v.tensor_tensor(onehot, over(idx[:], NB), bc(stat[:, 6, :], E), ALU.is_equal))

        def choose_two(v, ch, logits, first, second, tmp, s_diff, s_exp):
            choose(v, ch, logits, stat[:, 7, :], first, tmp)
            ch.link(v.tensor_scalar(tmp, first, -BIG, None, ALU.mult))
            ch.link(v.tensor_tensor(logits, logits, tmp, ALU.add))
            choose(v, ch, logits, stat[:, 8, :], second, tmp)
            v.tensor_tensor(stat[:, 9, :], stat[:, 8, :], stat[:, 7, :], ALU.subtract).then_inc(s_diff, 1)
            v.wait_ge(s_exp, 1)
            ch.link(v.tensor_scalar(stat[:, 10, :], stat[:, 9, :], 1.0, None, ALU.add))
            ch.link(v.reciprocal(stat[:, 8, :], stat[:, 10, :]))
            ch.link(v.tensor_tensor(stat[:, 9, :], stat[:, 9, :], stat[:, 8, :], ALU.mult))

        def ffn_inputs(layer):
            norm = Norm(f"ffn{layer}")
            s_xn, s_xt, s_xe, s_log, s_chain, s_th, s_xs, s_g = (
                sem("normed"), sem("turned"), sem("turned_copied"), sem("logits"), sem("vector_step"),
                sem("exponential"), sem("scaled"), sem("gates_ready"))
            s_diff, s_gt, s_b2 = sem("difference"), sem("gates_turned"), sem("bias_product")
            src = work2 if layer == 3 else xn[:]
            logits, first, second, tmp, tmp2 = slot(2), slot(3), slot(4), slot(5), slot(6)
            gT = work2[0:E].rearrange("p b d -> p (b d)")

            with nc.Block() as block:
                if layer == 0:
                    @block.sync
                    def _(sp):
                        for i, n in enumerate(("sh_gate", "sh_up")):
                            sp.dma_start(shw[:, i], a[n]).then_inc(s_w["misc"], 16)
                        sp.dma_start(shw[:, 2].rearrange("p (a d) -> p a d", a=2),
                                     a["sh_down"].rearrange("(a p) d -> p a d", p=P)).then_inc(s_w["misc"], 16)

                @block.vector
                def _(v):
                    ch = Chain(v, s_chain)
                    if layer == 3:
                        norm.vector(v, ch, xn[:], work2, 1e-6, centre=False)
                    else:
                        norm.vector(v, ch, x[:], xn[:], 1e-5)
                    v.drain().then_inc(s_xn, 1)
                    v.wait_ge(s_log, 1)
                    lg = ps[4][:, 0:P].rearrange("p (b e) -> p b e", e=E)
                    if layer == 3:
                        ch.link(v.tensor_tensor(logits, lg, over(rbias[:], NB), ALU.add))
                    else:
                        ch.link(v.tensor_copy(logits, lg))
                    if layer == 0:
                        choose(v, ch, logits, stat[:, 7, :], first, tmp)
                        v.tensor_scalar(gates[:, :, 0:E], first, 0.5, None, ALU.mult).then_inc(s_diff, 1)
                        v.wait_ge(s_th, 1)
                        ch.link(v.tensor_scalar(stat[:, 9, :], stat[:, 8, :], 0.5, 0.5, ALU.mult, ALU.add))
                        v.tensor_tensor(work2, xn[:], bc(stat[:, 9, :], P), ALU.mult).then_inc(s_xs, 1)
                    if layer == 2:
                        choose_two(v, ch, logits, first, second, tmp, s_diff, s_th)
                        ch.link(v.tensor_tensor(tmp, first, bc(stat[:, 8, :], E), ALU.mult))
                        ch.link(v.tensor_tensor(tmp2, second, bc(stat[:, 9, :], E), ALU.mult))
                        ch.link(v.tensor_tensor(tmp, tmp, tmp2, ALU.add))
                        v.tensor_scalar(gates[:, :, 0:E], tmp, 0.5, None, ALU.mult).then_inc(s_g, 1)
                    if layer == 3:
                        choose_two(v, ch, logits, first, second, tmp, s_diff, s_th)
                        both = rt[:, 8:10, :].rearrange("p s n -> p (s n)").rearrange("p (b k) -> p b k", k=16)
                        ch.link(v.tensor_copy(both[:, :, 0:E], first))
                        v.tensor_copy(both[:, :, E:16], second).then_inc(s_g, 1)
                        v.wait_ge(s_log, 2)
                        pads = [work[:, 1280:1280 + 24 * 16].rearrange("p (b k) -> p b k", k=16),
                                work[:, 1664:1664 + 24 * 16].rearrange("p (b k) -> p b k", k=16)]
                        total = ps[5][:, 256:512].rearrange("p (b k) -> p b k", k=16)
                        within = ps[5][:, 0:256].rearrange("p (b k) -> p b k", k=16)
                        ch.link(v.memset(pads[0][:, 0:8, :], 0.0))
                        ch.link(v.memset(pads[1][:, 0:8, :], 0.0))
                        ch.link(v.tensor_copy(pads[0][:, 8:24, :], total))
                        for i, step in enumerate((1, 2, 4, 8)):
                            p0, p1 = pads[i % 2], pads[1 - i % 2]
                            ch.link(v.tensor_tensor(p1[:, 8:24, :], p0[:, 8:24, :], p0[:, 8 - step:24 - step, :],
                                                    ALU.add))
                        pos = pads[1][:, 8:24, :]
                        ch.link(v.tensor_tensor(pos, pads[0][:, 8:24, :], total, ALU.subtract))
                        ch.link(v.tensor_tensor(pos, pos, within, ALU.add))
                        ch.link(v.tensor_tensor(pos[:, :, E:16], pos[:, :, E:16], pos[:, :, 0:E], ALU.add))
                        ch.link(v.tensor_scalar(pos, pos, float(CAP), None, ALU.is_lt))
                        ch.link(v.tensor_tensor(both, both, pos, ALU.mult))
                        kept = [stat[:, 10, :], stat[:, 11, :]]
                        for k in range(2):
                            m = both[:, :, k * E:(k + 1) * E]
                            ch.link(v.tensor_reduce(kept[k], m, AX_X, ALU.add))
                            ch.link(v.tensor_tensor(tmp, m, over(idx[:], NB), ALU.mult))
                            ch.link(v.tensor_reduce(stat[:, 6 + k, :], tmp, AX_X, ALU.add))
                            ch.link(v.tensor_scalar(stat[:, k, :], kept[k], -1.0, float(E), ALU.add, ALU.mult))
                            ch.link(v.tensor_scalar(stat[:, k, :], stat[:, k, :], -1.0, None, ALU.mult))
                            ch.link(v.tensor_tensor(stat[:, 6 + k, :], stat[:, 6 + k, :], stat[:, k, :], ALU.subtract))
                        ch.link(v.tensor_tensor(stat[:, 6, :], stat[:, 6, :], stat[:, 7, :], ALU.max))
                        ch.link(v.tensor_tensor(tmp, over(idx[:], NB), bc(stat[:, 6, :], E), ALU.is_equal))
                        for k in range(2):
                            ch.link(v.tensor_tensor(stat[:, k, :], stat[:, 8 + k, :], kept[k], ALU.mult))
                            ch.link(v.tensor_tensor(stat[:, 2 + k, :], stat[:, 8 + k, :], stat[:, k, :], ALU.subtract))
                        ch.link(v.tensor_tensor(stat[:, 0, :], stat[:, 0, :], stat[:, 1, :], ALU.add))
                        ch.link(v.tensor_tensor(stat[:, 2, :], stat[:, 2, :], stat[:, 3, :], ALU.add))
                        ch.link(v.tensor_tensor(gates[:, :, 0:E], tmp, bc(stat[:, 0, :], E), ALU.mult))
                        ch.link(v.tensor_tensor(work2, work2, over(b_row["g2"], NB), ALU.mult))
                        ch.link(v.tensor_tensor(work2, work2, bc(stat[:, 2, :], P), ALU.mult))
                        ch.link(v.tensor_tensor(xn[:], xn[:], work2, ALU.add))

                @block.gpsimd
                def _(g):
                    norm.gpsimd(g)
                    g.memset(gates[:, :, E:E + 1], 0.5)

                @block.tensor
                def _(pe):
                    pe.wait_ge(s_xn, 1)
                    for c in range(NC):
                        transposes(pe, src, c, c).then_inc(s_xt, 1)
                    pe.wait_ge(s_xe, NC)
                    for b in range(NB):
                        ins = pe.matmul(ps[4][:, b * E:(b + 1) * E], xT[:, b * P:(b + 1) * P],
                                        router[:, {0: 0, 2: 1, 3: 2}[layer], :], start=True, stop=True)
                    ins.then_inc(s_log, 1)
                    if layer == 0:
                        pe.wait_ge(s_xs, 1)
                        for c in range(NC):
                            transposes(pe, work2, c, c).then_inc(s_xt, 1)
                    if layer == 2:
                        pe.wait_ge(s_g, 1)
                        for c in range(NC):
                            for t in range(TPC):
                                ins = pe.transpose(ps[c][0:E, t * P:(t + 1) * P], tmp[:, c * TPC + t, :], ident[:])
                            ins.then_inc(s_xt, 1)
                        for c in range(NC):
                            pe.wait_ge(s_xe, NC + c + 1)
                            for t in range(TPC):
                                ins = pe.matmul(ps[4 + c][:, t * P:(t + 1) * P],
                                                gT[:, c * CH + t * P:c * CH + (t + 1) * P], b2[:],
                                                start=True, stop=True)
                            ins.then_inc(s_b2, 1)
                    if layer == 3:
                        both = rt[:, 8:10, :].rearrange("p s n -> p (s n)")
                        pe.wait_ge(s_g, 1)
                        pe.matmul(ps[5][:, 0:256], upto[:], both, start=True, stop=True)
                        pe.matmul(ps[5][:, 256:512], ones[:], both, start=True, stop=True).then_inc(s_log, 1)

                @block.scalar
                def _(s):
                    norm.scalar(s, xn[:])
                    for c in range(NC):
                        s.wait_ge(s_xt, c + 1)
                        if layer == 3:
                            s.activation(xT[:, c * CH:(c + 1) * CH], ps[c][:], ACT.Copy, scale=col["g2"])\
                                .then_inc(s_xe, 1)
                        else:
                            s.activation(xT[:, c * CH:(c + 1) * CH], ps[c][:], ACT.Copy).then_inc(s_xe, 1)
                    s.wait_ge(s_diff, 1)
                    if layer == 0:
                        s.activation(stat[:, 8, :], stat[:, 7, :], ACT.Tanh, scale=0.5).then_inc(s_th, 1)
                        for c in range(NC):
                            s.wait_ge(s_xt, NC + c + 1)
                            s.activation(kT[:, c * CH:(c + 1) * CH], ps[c][:], ACT.Copy).then_inc(s_xe, 1)
                    else:
                        s.activation(stat[:, 9, :], stat[:, 9, :], ACT.Exp).then_inc(s_th, 1)
                    if layer == 2:
                        for c in range(NC):
                            s.wait_ge(s_xt, NC + c + 1)
                            s.activation(gT[:, c * CH:(c + 1) * CH], ps[c][0:E, :], ACT.Copy).then_inc(s_xe, 1)
                        for c in range(NC):
                            s.wait_ge(s_b2, c + 1)
                            s.activation(xn[:, c * TPC:(c + 1) * TPC, :],
                                         ps[4 + c][:].rearrange("p (t d) -> p t d", t=TPC), ACT.Copy)\
                                .then_inc(s_xe, 1)

        def experts(layer, arena):
            order = ([E] if layer == 0 else []) + list(range(E))
            n = len(order)
            s_gu, s_act, s_a, s_free, s_h, s_y, s_acc, s_ch = (
                sem("up_products"), sem("activated"), sem("gated"), sem("banks_read"), sem("hidden"),
                sem("down_products"), sem("summed"), sem("chunk_step"))
            s_hid = s_h if layer == 3 else s_free
            hid = work[:, 0:2048].rearrange("p (k h n) -> p k h n", k=2, h=2)
            t_buf = work[:, 2048:3072].rearrange("p (h n) -> p h n", h=2)
            a_buf = work[:, 3072:4096].rearrange("p (h n) -> p h n", h=2)
            g_buf = pt[:]
            acc = q_s[:, 0, :].rearrange("p (t d) -> p t d", t=TPC)
            gch = q_s[:, 1, 0:TPC * (E + 1)].rearrange("p (t e) -> p t e", t=TPC)
            w_in = lambda m, e, h: (shw[:, m, h * P:(h + 1) * P] if e == E else arena[:, m, e, h * P:(h + 1) * P])

            with nc.Block() as block:
                @block.tensor
                def _(pe):
                    if layer == 0:
                        pe.wait_ge(s_w["a"], 16 * 3)
                        pe.wait_ge(s_w["misc"], 16 * 3)
                    if layer == 3:
                        pe.wait_ge(s_w["a3"], 16 * 3)

                    def down(c, k):
                        u = n * c + k
                        pe.wait_ge(s_hid, 2 * u + 3)
                        pe.wait_ge(s_acc, (u if k >= 2 else n * c + 1))
                        for t in range(TPC):
                            for h in range(HALVES):
                                ins = pe.matmul(ps[4 + k % 2][:, t * P:(t + 1) * P],
                                                hid[:, k % 2, h, t * P:(t + 1) * P], w_in(2, order[k], h),
                                                start=(h == 0), stop=(h == 1))
                        ins.then_inc(s_y, 1)

                    with pe.Fori(0, NC) as c:
                        for k, e in enumerate(order):
                            u = n * c + k
                            src = kT if layer == 0 and e != E else xT
                            for h in range(HALVES):
                                pe.wait_ge(s_free, 2 * u + h if k else 2 * n * c + 1)
                                for m in range(2):
                                    ins = pe.matmul(ps[2 * h + m][:], w_in(m, e, h), src[:, bass.ds(c * CH, CH)],
                                                    start=True, stop=True)
                                ins.then_inc(s_gu, 1)
                            if k:
                                down(c, k - 1)
                        down(c, n - 1)

                @block.scalar
                def _(s):
                    with s.Fori(0, NC) as c:
                        for k, e in enumerate(order):
                            u = n * c + k
                            for h in range(HALVES):
                                s.wait_ge(s_gu, 2 * u + h + 1)
                                if layer == 0:
                                    s.activation(t_buf[:, h, :], ps[2 * h][:], ACT.Tanh, scale=0.5).then_inc(s_act, 1)
                                if layer == 2:
                                    s.activation(t_buf[:, h, :], ps[2 * h][:], ACT.Tanh, scale=0.5,
                                                 bias=b1_half[:, e, h:h + 1])
                                    s.activation(g_buf[:, h, :], ps[2 * h][:], ACT.Identity,
                                                 bias=b1_cols[:, e, h:h + 1]).then_inc(s_act, 1)
                                if layer == 3:
                                    s.activation(t_buf[:, h, :], ps[2 * h][:], ACT.Copy).then_inc(s_act, 1)
                            if layer == 3:
                                for h in range(HALVES):
                                    s.wait_ge(s_free, 2 * u + h + 2)
                                    s.wait_ge(s_y, u if k >= 2 else n * c + 1)
                                    s.activation(hid[:, k % 2, h, :], a_buf[:, h, :], ACT.Gelu).then_inc(s_h, 1)

                @block.vector
                def _(v):
                    for q in (s_free, s_acc, s_y) + ((s_h,) if layer == 3 else ()):
                        v.drain().then_inc(q, 1)

                    def add_up(c, k):
                        u = n * c + k
                        e = order[k]
                        v.wait_ge(s_y, u + 2)
                        if layer == 0 and k == 0:
                            v.tensor_scalar(acc, ps[4][:].rearrange("p (t d) -> p t d", t=TPC), 0.5, None,
                                            ALU.mult).then_inc(s_acc, 1)
                            return
                        v.wait_ge(s_acc, u + 1)
                        for t in range(TPC):
                            ins = v.scalar_tensor_tensor(out=acc[:, t, :], in0=ps[4 + k % 2][:, t * P:(t + 1) * P],
                                                         scalar=gch[:, t, e:e + 1], in1=acc[:, t, :],
                                                         op0=ALU.mult, op1=ALU.add)
                        ins.then_inc(s_acc, 1)

                    with v.Fori(0, NC) as c:
                        v.tensor_copy(gch, gates[:, bass.ds(c * TPC, TPC), :]).then_inc(s_ch, 1)
                        if layer != 0:
                            v.tensor_copy(acc, xn[:, bass.ds(c * TPC, TPC), :]).then_inc(s_ch, 1)
                        v.wait_ge(s_ch, (2 if layer == 0 else 3) * c + (1 if layer == 0 else 2))
                        for k, e in enumerate(order):
                            u = n * c + k
                            for h in range(HALVES):
                                v.wait_ge(s_act, 2 * u + h + 1)
                                g_, u_ = ps[2 * h], ps[2 * h + 1]
                                if layer == 3:
                                    v.wait_ge(s_h, 2 * u + h if k else 2 * n * c + 1)
                                    v.tensor_tensor(a_buf[:, h, :], u_[:], t_buf[:, h, :], ALU.mult)\
                                        .then_inc(s_free, 1)
                                    continue
                                v.scalar_tensor_tensor(out=a_buf[:, h, :], in0=t_buf[:, h, :], scalar=1.0,
                                                       in1=g_[:] if layer == 0 else g_buf[:, h, :],
                                                       op0=ALU.add, op1=ALU.mult).then_inc(s_a, 1)
                                v.wait_ge(s_a, 2 * u + h + 1)
                                v.wait_ge(s_y, u if k >= 2 else n * c + 1)
                                if layer == 0:
                                    ins = v.tensor_tensor(hid[:, k % 2, h, :], u_[:], a_buf[:, h, :], ALU.mult)
                                else:
                                    ins = v.scalar_tensor_tensor(out=hid[:, k % 2, h, :], in0=u_[:],
                                                                 scalar=b3_cols[:, e, h:h + 1],
                                                                 in1=a_buf[:, h, :], op0=ALU.add, op1=ALU.mult)
                                ins.then_inc(s_free, 1)
                            if k:
                                add_up(c, k - 1)
                        add_up(c, n - 1)
                        v.wait_ge(s_acc, n * c + n + 1)
                        xc = x[:, bass.ds(c * TPC, TPC), :]
                        v.scalar_tensor_tensor(out=xc.rearrange("p t d -> p (t d)"), in0=q_s[:, 0, :],
                                               scalar=tg["f", layer], in1=xc.rearrange("p t d -> p (t d)"),
                                               op0=ALU.mult, op1=ALU.add).then_inc(s_ch, 1)
                        v.wait_ge(s_ch, (2 if layer == 0 else 3) * (c + 1))

        def l1_inputs():
            norm = Norm("l1")
            s_xn, s_xt, s_xe, s_chain, s_m = (sem("normed"), sem("turned"), sem("turned_copied"),
                                              sem("vector_step"), sem("mask_made"))
            with nc.Block() as block:
                @block.sync
                def _(sp):
                    for i, n in enumerate(("l3_w1", "l3_w2")):
                        sp.dma_start(arena_a[:, i], a[n].rearrange("e h i -> h e i")).then_inc(s_w["a3"], 16)
                    sp.dma_start(arena_a[:, 2].rearrange("p e (a d) -> p e a d", a=2),
                                 a["l3_w3"].rearrange("e (a p) d -> p e a d", p=P)).then_inc(s_w["a3"], 16)

                @block.vector
                def _(v):
                    ch = Chain(v, s_chain)
                    norm.vector(v, ch, ctx_tok[:], v_tok[:], 1e-5)
                    v.drain().then_inc(s_xn, 1)
                    norm.vector(v, ch, x[:], xn[:], 1e-5)
                    norm.vector(v, ch, xn[:], xn[:], 1e-5)
                    v.drain().then_inc(s_xn, 1)

                @block.gpsimd
                def _(g):
                    for _ in range(3):
                        norm.gpsimd(g)
                    zero_values(g)
                    g.wait_ge(s_xt, 2 * NC)
                    g.tensor_copy(xn[:], m8[:].bitcast(U8)).then_inc(s_m, 1)
                    g.wait_ge(s_m, 1)
                    g.tensor_scalar(xn[:], xn[:], -1.0, BIG, ALU.add, ALU.mult)

                @block.tensor
                def _(pe):
                    pe.wait_ge(s_w["att"], 16 * 5)
                    for i, src in enumerate((v_tok, xn)):
                        pe.wait_ge(s_xn, i + 1)
                        for c in range(NC):
                            transposes(pe, src[:], 4 * i + c, c).then_inc(s_xt, 1)

                @block.scalar
                def _(s):
                    def copies(i):
                        dst, g_, b_ = ((kT, "lnx_g", "lnx_b"), (qT, "lnl_g", "lnl_b"))[i]
                        for c in range(NC):
                            s.wait_ge(s_xt, i * NC + c + 1)
                            s.activation(dst[:, c * CH:(c + 1) * CH], ps[4 * i + c][:], ACT.Identity,
                                         scale=col[g_], bias=col[b_]).then_inc(s_xe, 1)

                    norm.scalar(s, v_tok[:])
                    norm.scalar(s, xn[:])
                    norm.scalar(s, xn[:])
                    copies(0)
                    copies(1)

        class HeadsL1:
            heads = 2
            tiles = 4
            scale = 1.0 / 64
            out_banks = 2
            scalar_sums = False
            dve_fronts = ()

            def mask(self, bank, b):
                return bank[:, :, 0:P], xn[:, bass.ds(b, 1), :].broadcast_to([P, 2, P])

            def setup(self):
                self.s_stage, self.s_f, self.s_fe = sem("inputs_staged"), sem("items"), sem("items_copied")

            def scores(self, pe, bank, par, g):
                return pe.matmul(bank[:], q_s[:, par, g * P:(g + 1) * P],
                                 kv[:, par * 2048 + g * CH:par * 2048 + (g + 1) * CH], start=True, stop=True)

            def pv(self, pe, par, g, pt_g):
                for j in range(4):
                    head, kc = 2 * g + j // 2, j % 2
                    at = 4096 + par * 2048 + (kc * 8 + head) * P
                    ins = pe.matmul(ps[4 + par][:, g * P:(g + 1) * P], kv[:, at:at + P], pt_g[:, j * P:(j + 1) * P],
                                    start=(j == 0), stop=(j == 3))
                return ins

            def out_w(self, t):
                return l1o[:, t, :]

            def scores_ready(self, pe, b, g):
                if g % 2 == 0:
                    pe.wait_ge(self.s_fe, 5 * b + 2 + g // 2)

            def out_bank(self, par, k):
                return ps[4 + par]

            @property
            def pool_fronts(self):
                return ((2, 3, self.stage_inputs),)

            @property
            def pe_fronts(self):
                return ((0, 0, self.item(3)), (0, 1, self.item(4)),
                        (1, 1, self.item(0)), (1, 2, self.item(1)), (1, 3, self.item(2)))

            @property
            def act_fronts(self):
                return ((0, 0, self.copy(2)), (0, 1, self.copy(3)), (0, 2, self.copy(4)),
                        (1, 2, self.copy(0)), (1, 3, self.copy(1)))

            def values_ready(self, pe, b):
                pe.wait_ge(self.s_fe, 5 * b + 5)

            def bank(self, par, j):
                return ps[6 + (par + j) % 2]

            def stage_inputs(self, gp, n, par, first, cnt):
                if not first:
                    gp.wait_ge(self.s_f, 5 * (n - 1))
                gp.tensor_copy(stage[:, par, 0:P], kT[:, bass.ds(n * P, P)]).then_inc(self.s_stage, 1)
                gp.tensor_copy(stage[:, par, P:2 * P], qT[:, bass.ds(n * P, P)]).then_inc(self.s_stage, 1)

            def item(self, j):
                def f(pe, n, par, first, cnt):
                    bank = self.bank(par, j)
                    if j == 0:
                        pe.wait_ge(self.s_stage, 2 * n + 2)
                    if not (isinstance(n, int) and 5 * n + j < 2):
                        pe.wait_ge(self.s_fe, 5 * n + j - 1)
                    if j == 0:
                        for t in range(4):
                            ins = pe.matmul(bank[:, t * P:(t + 1) * P], l1q[:, t * P:(t + 1) * P],
                                            stage[:, par, P:2 * P], start=True, stop=True)
                    elif j < 3:
                        for t in range(2):
                            at = (2 * (j - 1) + t) * P
                            ins = pe.matmul(bank[:, t * 256:(t + 1) * 256], l1kv[:, at:at + P],
                                            stage[:, par, :], start=True, stop=True)
                    else:
                        ins = pe.matmul(bank[:], stage[:, par, (j - 3) * P:(j - 2) * P], l1kv[:, 512:1024],
                                        start=True, stop=True)
                    ins.then_inc(self.s_f, 1)
                return f

            def copy(self, j):
                def f(s, n, par, first, cnt):
                    bank = self.bank(par, j)
                    s.wait_ge(self.s_f, 5 * n + j + 1)
                    if j == 0:
                        if not first:
                            s.wait_ge(cnt["scores"], 4 * (n - 1))
                        ins = s.activation(q_s[:, par, :], bank[:], ACT.Copy)
                    elif j < 3:
                        for m in range(2):
                            at = par * 2048 + 2 * (j - 1) * CH + m * 256
                            ins = s.activation(strided(kv[:, at:at + 256], [(CH, 2), (1, 256)]),
                                               bank[:].rearrange("p (t k) -> p t k", t=2), ACT.Copy,
                                               scale=mask2[:, m:m + 1])
                    else:
                        if j == 3 and not first:
                            s.wait_ge(cnt["pv"], 4 * (n - 1))
                        at = 4096 + par * 2048 + (j - 3) * 1024
                        ins = s.activation(strided(kv[:, at:at + 1024], [(256, 4), (192, 2), (1, 64)]),
                                           bank[:].rearrange("p (t m d) -> p t m d", t=4, m=2), ACT.Copy)
                    ins.then_inc(self.s_fe, 1)
                return f

        def l1_after():
            norm = Norm("l1_after")
            s_xn, s_xt, s_chain, s_max, s_wq, s_bias, s_wt = (
                sem("quantised"), sem("turned"), sem("vector_step"), sem("largest"), sem("weights_quantised"),
                sem("bias_added"), sem("weights_turned"))
            with nc.Block() as block:
                @block.vector
                def _(v):
                    ch = Chain(v, s_chain)
                    norm.vector(v, ch, v_tok[:], v_tok[:], 1e-5)
                    ch.link(v.tensor_tensor(v_tok[:], v_tok[:], over(b_row["lno_g"], NB), ALU.mult))
                    ch.link(v.tensor_tensor(v_tok[:], v_tok[:], over(b_row["lno_b"], NB), ALU.add))
                    ch.link(v.scalar_tensor_tensor(out=flat(x), in0=flat(v_tok), scalar=tg["x", 1], in1=flat(x),
                                                   op0=ALU.mult, op1=ALU.add))
                    norm.vector(v, ch, x[:], xn[:], 1e-5)
                    v.tensor_reduce(tiny[:, 0:1], flat(xn), AX_X, ALU.max, apply_absolute_value=True)\
                        .then_inc(s_max, 1)
                    v.wait_ge(s_w["att"], 16 * 5)
                    for w, o in ((winT, 8), (wout, 16)):
                        ch.link(v.tensor_reduce(tiny[:, o:o + 4], w, AX_X, ALU.max, apply_absolute_value=True))
                        scales(v, ch, o, 4, 127.0)
                        for g in range(4):
                            quantise(v, ch, w[:, g, :], w[:, g, :], tiny[:, o + 4 + g:o + 5 + g],
                                     tiny[:, o + g:o + g + 1], -128.0, 127.0)
                        v.drain().then_inc(s_wq, 1)
                    v.wait_ge(s_max, 2)
                    scales(v, ch, 1, 1, 32767.0)
                    quantise(v, ch, flat(xn), flat(xn), tiny[:, 2:3], tiny[:, 1:2], -32768.0, 32767.0)
                    v.drain().then_inc(s_xn, 1)

                @block.gpsimd
                def _(g):
                    norm.gpsimd(g)
                    norm.gpsimd(g)
                    g.wait_ge(s_max, 1)
                    g.partition_all_reduce(tiny[:, 1:2], tiny[:, 0:1], P, RMAX).then_inc(s_max, 1)
                    g.tensor_scalar(bo1_row[:], bo1_row[:], tg["f", 1], None, ALU.mult).then_inc(s_bias, 1)
                    g.wait_ge(s_bias, 1)
                    g.tensor_tensor(x[:], x[:], over(bo1_row[:], NB), ALU.add)

                @block.tensor
                def _(pe):
                    pe.wait_ge(s_wq, 1)
                    for g in range(4):
                        ins = pe.transpose(ps[4][:, g * P:(g + 1) * P], winT[:, g, :], ident[:])
                    ins.then_inc(s_wt, 1)
                    pe.wait_ge(s_xn, 1)
                    for c in range(NC):
                        transposes(pe, xn[:], c, c).then_inc(s_xt, 1)

                @block.scalar
                def _(s):
                    norm.scalar(s, v_tok[:])
                    norm.scalar(s, xn[:])
                    s.wait_ge(s_wt, 1)
                    s.activation(win_q, ps[4][:], ACT.Copy)
                    for c in range(NC):
                        s.wait_ge(s_xt, c + 1)
                        s.activation(xT[:, c * CH:(c + 1) * CH], ps[c][:], ACT.Copy)

        def scales(v, ch, o, n, top):
            m, r = tiny[:, o:o + n], tiny[:, o + n:o + 2 * n]
            ch.link(v.tensor_scalar(m, m, 1e-8, None, ALU.max))
            ch.link(v.reciprocal(r, m))
            ch.link(v.tensor_scalar(r, r, top, None, ALU.mult))
            ch.link(v.tensor_scalar(m, m, 1.0 / top, None, ALU.mult))

        def quantise(v, ch, dst, src, scale, inverse, low, high):
            ch.link(v.tensor_scalar(dst, src, scale, ROUND, ALU.mult, ALU.add))
            ch.link(v.tensor_scalar(dst, dst, ROUND, high, ALU.subtract, ALU.min))
            ch.link(v.tensor_scalar(dst, dst, low, inverse, ALU.max, ALU.mult))

        def l1_hidden():
            s_h, s_g, s_m, s_all, s_chain = (sem("hidden_products"), sem("hidden"), sem("largest_in_tile"),
                                             sem("largest"), sem("vector_step"))
            hidden = kv[:].rearrange("p (g n) -> p g n", g=4)
            with nc.Block() as block:
                @block.tensor
                def _(pe):
                    with pe.Fori(0, NC) as c:
                        for g in range(4):
                            pe.wait_ge(s_g, 4 * c + g - 3 + 4)
                            pe.matmul(ps[g][:], win_q[:, g * P:(g + 1) * P], xT[:, bass.ds(c * CH, CH)],
                                      start=True, stop=True).then_inc(s_h, 1)

                @block.scalar
                def _(s):
                    for _ in range(4):
                        s.drain().then_inc(s_g, 1)
                    with s.Fori(0, NC) as c:
                        for g in range(4):
                            s.wait_ge(s_h, 4 * c + g + 1)
                            s.activation(hidden[:, g, bass.ds(c * CH, CH)], ps[g][:], ACT.Gelu,
                                         bias=col[f"b_in{g}"]).then_inc(s_g, 1)

                @block.vector
                def _(v):
                    with v.Fori(0, NC) as c:
                        for g in range(4):
                            v.wait_ge(s_g, 4 * c + g + 1 + 4)
                            v.tensor_reduce(tiny[:, bass.ds(16 + 4 * c + g, 1)], hidden[:, g, bass.ds(c * CH, CH)],
                                            AX_X, ALU.max, apply_absolute_value=True).then_inc(s_m, 1)
                    v.wait_ge(s_m, 16)
                    v.tensor_reduce(tiny[:, 0:1], tiny[:, 16:32], AX_X, ALU.max).then_inc(s_all, 1)
                    v.wait_ge(s_all, 2)
                    scales(v, Chain(v, s_chain), 1, 1, 32767.0)

                @block.gpsimd
                def _(g):
                    g.wait_ge(s_all, 1)
                    g.partition_all_reduce(tiny[:, 1:2], tiny[:, 0:1], P, RMAX).then_inc(s_all, 1)

        def l1_output():
            s_q, s_y, s_x, s_chain = sem("hidden_quantised"), sem("products"), sem("added"), sem("vector_step")
            hidden = kv[:].rearrange("p (g n) -> p g n", g=4)
            hq = [work[:, i * 2048:(i + 1) * 2048].rearrange("p (g n) -> p g n", g=4) for i in range(2)]
            with nc.Block() as block:
                @block.sync
                def _(sp):
                    sp.dma_start(xT[:, 0:P], a["bv_cols"]).then_inc(s_w["misc"], 16)

                @block.vector
                def _(v):
                    ch = Chain(v, s_chain)

                    def add(c):
                        v.wait_ge(s_y, c + 1)
                        xc = x[:, c * TPC:(c + 1) * TPC, :].rearrange("p t d -> p (t d)")
                        v.scalar_tensor_tensor(out=xc, in0=ps[c % 2][:], scalar=tg["f", 1], in1=xc,
                                               op0=ALU.mult, op1=ALU.add).then_inc(s_x, 1)

                    for c in range(NC):
                        if c >= 2:
                            v.wait_ge(s_y, c - 1)
                        quantise(v, ch, hq[c % 2], hidden[:, :, c * CH:(c + 1) * CH], tiny[:, 2:3], tiny[:, 1:2],
                                 -32768.0, 32767.0)
                        v.drain().then_inc(s_q, 1)
                        if c:
                            add(c - 1)
                    add(NC - 1)

                @block.tensor
                def _(pe):
                    for c in range(NC):
                        pe.wait_ge(s_q, c + 1)
                        if c >= 2:
                            pe.wait_ge(s_x, c - 1)
                        for t in range(TPC):
                            for g in range(4):
                                ins = pe.matmul(ps[c % 2][:, t * P:(t + 1) * P], hq[c % 2][:, g, t * P:(t + 1) * P],
                                                wout[:, g, :], start=(g == 0), stop=(g == 3))
                        ins.then_inc(s_y, 1)

        def l3_inputs():
            norm, rms = Norm("l3_ffn"), Norm("l3_rms")
            s_xn, s_xt, s_chain = sem("normed"), sem("turned"), sem("vector_step")
            with nc.Block() as block:
                @block.vector
                def _(v):
                    ch = Chain(v, s_chain)
                    norm.vector(v, ch, x[:], xn[:], 1e-5)
                    rms.vector(v, ch, xn[:], work2, 1e-6, centre=False)
                    v.drain().then_inc(s_xn, 1)

                @block.gpsimd
                def _(g):
                    norm.gpsimd(g)
                    rms.gpsimd(g)
                    g.wait_ge(s_w["att3"], 16 * 4)
                    for w, r, n in ((l3q, l3q_rot, 16), (l3k, l3k_rot, 4)):
                        w3 = w.rearrange("p (n d) -> p n d", n=n)
                        r3 = r.rearrange("p (n d) -> p n d", n=n)
                        g.tensor_scalar(r3[:, :, 0:32], w3[:, :, 32:64], -1.0, None, ALU.mult)
                        g.tensor_copy(r3[:, :, 32:64], w3[:, :, 0:32])
                    zero_values(g)

                @block.tensor
                def _(pe):
                    pe.wait_ge(s_xn, 1)
                    for c in range(NC):
                        transposes(pe, work2, c, c).then_inc(s_xt, 1)

                @block.scalar
                def _(s):
                    norm.scalar(s, xn[:])
                    rms.scalar(s, xn[:])
                    for c in range(NC):
                        s.wait_ge(s_xt, c + 1)
                        s.activation(xT[:, c * CH:(c + 1) * CH], ps[c][:], ACT.Copy, scale=col["g1"])

        class HeadsL3:
            heads = 4
            tiles = 8
            scale = 64 ** -0.5
            out_banks = 1
            scalar_sums = True

            def mask(self, bank, b):
                return bank, over(causal[:], 4)

            def setup(self):
                self.s_stage, self.s_f, self.s_fv, self.s_fa, self.s_k, self.s_q, self.s_step = (
                    sem("inputs_staged"), sem("items"), sem("items_read"), sem("values_placed"),
                    sem("keys_masked"), sem("queries"), sem("rotary_step"))

            def q(self, par):
                return kv[:, par * 2048:par * 2048 + 1024]

            def km(self, par):
                return kv[:, par * 2048 + 1024:par * 2048 + 1536].rearrange("p (t m k) -> p t m k", t=2, m=2)

            def temps(self, par, i):
                if i == 0:
                    return q_s[:, 0, :], q_s[:, 1, :]
                return (kv[:, par * 2048 + 1536:(par + 1) * 2048],
                        kv[:, 4096 + par * 2048 + 1024:4096 + par * 2048 + 1536])

            def scores(self, pe, bank, par, g):
                for i in range(2):
                    at = par * 2048 + 1024 + i * 256
                    ins = pe.matmul(bank[:, i * 256:(i + 1) * 256], self.q(par)[:, (2 * g + i) * P:(2 * g + i + 1) * P],
                                    kv[:, at:at + 256], start=True, stop=True)
                return ins

            def pv(self, pe, par, g, pt_g):
                for j in range(4):
                    t, m = 2 * g + j // 2, j % 2
                    at = 4096 + par * 2048 + j * P
                    ins = pe.matmul(ps[4 + t // 4][:, (t % 4) * P:(t % 4 + 1) * P], kv[:, at:at + P],
                                    pt_g[:, j * P:(j + 1) * P], start=(m == 0), stop=(m == 1))
                return ins

            def out_w(self, t):
                return l3o[:, t, :]

            def scores_ready(self, pe, b, g):
                if g == 0:
                    pe.wait_ge(self.s_k, b + 1)
                if g % 2 == 0:
                    pe.wait_ge(self.s_q, 2 * b + 1 + g // 2)

            def out_bank(self, par, k):
                return ps[4 + k]

            @property
            def pool_fronts(self):
                return ((2, 3, self.stage_inputs), (1, 2, self.add_queries(0)), (1, 3, self.add_queries(1)))

            @property
            def pe_fronts(self):
                return ((1, 0, self.item(0)), (1, 1, self.item(1)), (1, 1, self.item(2)),
                        (1, 2, self.item(3)), (1, 2, self.item(4)), (1, 3, self.item(5)))

            @property
            def dve_fronts(self):
                return ((1, 1, self.keys), (1, 2, self.rotary(1)), (1, 2, self.rotary(2)),
                        (1, 3, self.rotary(3)), (1, 3, self.rotary(4)))

            @property
            def act_fronts(self):
                return ((0, 1, self.place_values),)

            def values_ready(self, pe, b):
                pe.wait_ge(self.s_fa, b + 1)

            def stage_inputs(self, gp, n, par, first, cnt):
                if not first:
                    gp.wait_ge(self.s_f, 6 * (n - 1))
                gp.tensor_copy(stage[:, par, 0:P], xT[:, bass.ds(n * P, P)]).then_inc(self.s_stage, 1)

            def add_queries(self, i):
                def f(gp, n, par, first, cnt):
                    t1, t2 = self.temps(par, i)
                    gp.wait_ge(self.s_fv, 5 * n + 3 + 2 * i)
                    if i == 0 and not first:
                        gp.wait_ge(cnt["scores"], 4 * (n - 1))
                    gp.tensor_tensor(self.q(par)[:, i * CH:(i + 1) * CH], t1, t2, ALU.add).then_inc(self.s_q, 1)
                return f

            def item(self, j):
                def f(pe, n, par, first, cnt):
                    bank = ps[6 + j % 2]
                    x_b = stage[:, par, 0:P]
                    start = isinstance(n, int) and n == 0
                    if j == 0:
                        pe.wait_ge(self.s_stage, n + 1)
                        if not start:
                            pe.wait_ge(self.s_fv, 5 * n)
                        for t in range(4):
                            w = (l3k, l3k_rot)[t // 2]
                            ins = pe.matmul(bank[:, t * P:(t + 1) * P], w[:, (t % 2) * P:(t % 2 + 1) * P], x_b,
                                            start=True, stop=True)
                    elif j < 5:
                        if j > 1:
                            pe.wait_ge(self.s_fv, 5 * n + j - 1)
                        elif not start:
                            pe.wait_ge(self.s_fa, n)
                        w = (l3q, l3q_rot)[(j - 1) % 2]
                        for t in range(4):
                            at = ((j - 1) // 2 * 4 + t) * P
                            ins = pe.matmul(bank[:, t * P:(t + 1) * P], w[:, at:at + P], x_b, start=True, stop=True)
                    else:
                        pe.wait_ge(self.s_fv, 5 * n + 4)
                        ins = pe.matmul(bank[:, 0:256], x_b, l3v, start=True, stop=True)
                    ins.then_inc(self.s_f, 1)
                return f

            def keys(self, v, n, par, first, cnt):
                bank = ps[6]
                at = 4096 + par * 2048 + 1536
                k1, k2 = kv[:, at:at + 256], kv[:, at + 256:at + 512]
                tile2 = lambda ap: ap.rearrange("p (t k) -> p t k", t=2)
                v.wait_ge(self.s_f, 6 * n + 1)
                v.tensor_tensor(tile2(k1), tile2(bank[:, 0:256]), over(cosT[:], 2), ALU.mult)
                v.tensor_tensor(tile2(k2), tile2(bank[:, 256:512]), over(sinT[:], 2), ALU.mult)\
                    .then_inc(self.s_fv, 1)
                v.wait_ge(self.s_fv, 5 * n + 1)
                v.tensor_tensor(k1, k1, k2, ALU.add).then_inc(self.s_step, 1)
                v.wait_ge(self.s_step, n + 1)
                if not first:
                    v.wait_ge(cnt["scores"], 4 * (n - 1))
                for m in range(2):
                    ins = v.tensor_scalar(self.km(par)[:, :, m, :], tile2(k1), mask2[:, m:m + 1], None, ALU.mult)
                ins.then_inc(self.s_k, 1)

            def rotary(self, j):
                def f(v, n, par, first, cnt):
                    bank = ps[6 + j % 2]
                    v.wait_ge(self.s_f, 6 * n + j + 1)
                    if j == 1 and not (isinstance(n, int) and n == 0):
                        v.wait_ge(self.s_q, 2 * n - 1)
                    dst = self.temps(par, (j - 1) // 2)[(j - 1) % 2]
                    tab = (cosT, sinT)[(j - 1) % 2]
                    v.tensor_tensor(dst.rearrange("p (t k) -> p t k", t=4),
                                    bank[:].rearrange("p (t k) -> p t k", t=4), over(tab[:], 4), ALU.mult)\
                        .then_inc(self.s_fv, 1)
                return f

            def place_values(self, s, n, par, first, cnt):
                s.wait_ge(self.s_f, 6 * n + 6)
                if not first:
                    s.wait_ge(cnt["pv"], 4 * (n - 1))
                at = 4096 + par * 2048
                s.activation(strided(kv[:, at:at + 512], [(256, 2), (192, 2), (1, 64)]),
                             ps[7][:, 0:256].rearrange("p (t m d) -> p t m d", t=2, m=2), ACT.Copy)\
                    .then_inc(self.s_fa, 1)

        def load_att3():
            with nc.Block() as block:
                @block.sync
                def _(sp):
                    for dst, n in ((l3q, "l3_wq"), (l3k, "l3_wk"), (l3v, "l3_wv")):
                        sp.dma_start(dst, a[n]).then_inc(s_w["att3"], 16)
                    sp.dma_start(l3o, a["l3_wo"].rearrange("(t p) d -> p t d", p=P)).then_inc(s_w["att3"], 16)

        def finish():
            s_out = sem("stored")
            with nc.Block() as block:
                @block.sync
                def _(sp):
                    sp.dma_start(out.rearrange("b p d -> p b d"), x[:]).then_inc(s_out, 16)
                    sp.wait_ge(s_out, 16)
                    for q_, n_ in (("a", 48), ("att", 80), ("a3", 48), ("att3", 64), ("misc", 64)):
                        sp.wait_ge(s_w[q_], n_)

        attention_inputs(0)
        spec = Heads16(0, float(P) ** -0.5, v_tok, lambda t: w_sq["l0o"])
        add_to(spec, x, tg["x", 0])
        attention(spec)
        ffn_inputs(0)
        experts(0, arena_a)
        l1_inputs()
        spec = HeadsL1()
        add_to(spec, v_tok)
        attention(spec)
        l1_after()
        l1_hidden()
        l1_output()
        recycle()
        load_att3()
        attention_inputs(2)
        l2_heads()
        spec = Heads16(2, 8 ** -0.5, v_tok, lambda t: w_sq["l2o"])
        add_to(spec, x, tg["x", 2])
        attention(spec)
        ffn_inputs(2)
        experts(2, arena_b)
        recycle()
        attention_inputs(3)
        spec = Heads16(3, 8 ** -0.5, ctx_tok, lambda t: ident[:])
        add_to(spec, x, tg["x", 3])
        attention(spec)
        l3_inputs()
        spec = HeadsL3()
        add_to(spec, xn, 1)
        attention(spec)
        ffn_inputs(3)
        experts(3, arena_a)
        finish()


_OUTS = [((NB, P, P), "float32")]


def layout(i):
    f = {k: np.asarray(v) for k, v in i.items()}

    def blocks(w):
        z = np.zeros((P, P), w.dtype)
        for h in range(16):
            z[8 * h:8 * h + 8, 8 * h:8 * h + 8] = w
        return z

    def row(v):
        return np.broadcast_to(v, (P, v.shape[-1]))

    d = dict(constants())
    d["x"] = f["x"]
    d["ctx"] = f["ctx_1024"]
    d["ctxT"] = f["ctx_1024"].transpose(2, 0, 1).reshape(P, T)
    d["mask8"] = np.broadcast_to(f["mask_BxS2_bk1"].view(np.int32).reshape(1, NB, P // 4), (P, NB, P // 4))
    d["gate_cols"] = np.broadcast_to(np.concatenate([f["g_xattn"], f["g_ffn"]]), (P, 8))
    d["squares"] = np.stack([
        blocks(f["L0_xattn_Wq"].T), blocks(f["L0_xattn_Wk"].T), blocks(f["L0_xattn_Wv"].T), f["L0_xattn_Wo"].T,
        f["L2_xattn_Wq"].T, f["L2_xattn_Wkv"][:P].T, f["L2_xattn_Wkv"][P:].T, f["L2_xattn_Wproj"].T])
    d["bias_rows"] = np.stack([row(f["L0_xattn_bo"]), row(f["L2_xattn_bq"]), row(f["L2_xattn_bkv"][:P]),
                               row(f["L2_xattn_bproj"]), row(f["L1_xattn_ln_o_g"]), row(f["L1_xattn_ln_o_b"]),
                               row(f["L3_ffn_g2"])], 1)
    d["bv_cols"] = np.broadcast_to(f["L2_xattn_bkv"][P:, None], (P, P))
    d["cols"] = np.stack([f["L1_xattn_ln_x_g"], f["L1_xattn_ln_x_b"], f["L1_xattn_ln_l_g"], f["L1_xattn_ln_l_b"]]
                         + [np.tile(f["L2_xattn_" + n], 16) for n in ("q_gamma", "q_beta", "k_gamma", "k_beta")]
                         + [f["L3_ffn_g1"], f["L3_ffn_g2"]] + [f["L1_ffn_b_in"][P * g:P * g + P] for g in range(4)], 1)
    d["bo1"] = row(f["L1_ffn_b_out"])
    d["rbias"] = row(f["L3_ffn_router_b"])
    d["router"] = np.stack([f["L0_ffn_gate_w"], f["L2_ffn_Wg"].T, f["L3_ffn_router_w"]], 1)
    d["l2_b2"] = f["L2_ffn_b2"]
    d["b1c"] = f["L2_ffn_b1"].reshape(E, 2, P).transpose(2, 0, 1)
    d["b3c"] = f["L2_ffn_b3"].reshape(E, 2, P).transpose(2, 0, 1)
    d["l0_gate"], d["l0_up"], d["l0_down"] = (f["L0_ffn_rt_" + n] for n in ("gate", "up", "down"))
    d["sh_gate"], d["sh_up"], d["sh_down"] = (f["L0_ffn_sh_" + n] for n in ("gate", "up", "down"))
    d["l1_wq"], d["l1_wkv"], d["l1_wo"] = (f["L1_xattn_" + n] for n in ("Wq", "Wkv", "Wo"))
    d["l1_winT"], d["l1_wout"] = f["L1_ffn_W_in"].T, f["L1_ffn_W_out"]
    d["l2_w1T"] = f["L2_ffn_W1"].transpose(2, 0, 1)
    d["l2_w3T"] = f["L2_ffn_W3"].transpose(2, 0, 1)
    d["l2_w2T"] = f["L2_ffn_W2"].reshape(E, P, 2, P).transpose(3, 0, 2, 1).reshape(P, E, 256)
    d["l2_a1"] = f["L2_ffn_A1"].transpose(1, 0, 2).reshape(16, E * P)
    d["l2_a3"] = f["L2_ffn_A3"].transpose(1, 0, 2).reshape(16, E * P)
    d["l2_a2"] = f["L2_ffn_A2"].transpose(1, 0, 2).reshape(16, E * 256)
    d["l2_b1T"] = f["L2_ffn_B1"].transpose(2, 0, 1).reshape(16, E * 256)
    d["l2_b3T"] = f["L2_ffn_B3"].transpose(2, 0, 1).reshape(16, E * 256)
    d["l2_b2T"] = f["L2_ffn_B2"].transpose(2, 0, 1).reshape(16, E * P)
    for n in ("wq", "wk", "wv", "wo", "w1", "w2", "w3"):
        d["l3_" + n] = f["L3_ffn_" + n]
    return {k: np.ascontiguousarray(v) for k, v in d.items()}


def kernel(**inputs):
    import concourse.bacc as _bacc
    from concourse import mybir as _mybir
    from concourse.bass_utils import run_bass_kernel_spmd as _run

    nc = _bacc.Bacc("TRN2", target_bir_lowering=False, num_devices=1)
    arrays, args = {}, {}
    for name, v in layout(inputs).items():
        arrays[f"in_{name}_dram"] = v
        args[name] = nc.dram_tensor(f"in_{name}_dram", v.shape, _mybir.dt.from_np(v.dtype), kind="ExternalInput").ap()
    shape, dtype = _OUTS[0]
    out = nc.dram_tensor("out_0_dram", shape, _mybir.dt.from_np(np.dtype(dtype)), kind="ExternalOutput").ap()
    build(nc, args, out)
    r = _run(nc, [arrays], core_ids=[0])
    return r.results[0]["out_0_dram"]
```
